# Optimizing a Trainium2 kernel written in Bass

```python
import numpy as np
import jax
import jax.numpy as jnp

def _softmax(x, axis=-1):
    return jax.nn.softmax(x, axis=axis)

def _gelu(x):
    return jax.nn.gelu(x, approximate=True)

def _silu(x):
    return jax.nn.silu(x)

def _sigmoid(x):
    return jax.nn.sigmoid(x)

def _layernorm(x, axis=-1, eps=1e-05):
    m = jnp.mean(x, axis=axis, keepdims=True)
    v = jnp.var(x, axis=axis, keepdims=True)
    return (x - m) / jnp.sqrt(v + eps)

def _scatter_add(tgt, idx, src, axis=0):
    return tgt.at[idx].add(src)

def _segment_sum(src, seg, n):
    return jax.ops.segment_sum(src, seg, n)
kernel_name = 'mk_prb_d1_jaxref_r4_aa847f'

def setup_inputs(seed: int=0):
    np.random.seed(seed)
    _w = jnp.asarray

    def _L0_attn_setup():
        import jax, jax.numpy as jnp
        import numpy as np
        import math
        THETA = 500.0
        SCALE = 1.0
        NUM_HEADS = 16

        def apply_rope(t, theta=THETA, scale=SCALE):
            D = t.shape[-1]
            L = t.shape[-2]
            half = D // 2
            freqs = 1.0 / theta ** (jnp.arange(half, dtype=jnp.float32) / half)
            angles = scale * jnp.arange(L, dtype=jnp.float32)[:, None] * freqs[None, :]
            cos = jnp.cos(angles)
            sin = jnp.sin(angles)
            t1, t2 = (t[..., :half], t[..., half:])
            return jnp.concatenate([t1 * cos - t2 * sin, t1 * sin + t2 * cos], axis=-1)
        key = jax.random.key(seed)
        k1, k2, k3 = jax.random.split(key, 3)
        B, L, Dm = (2, 1024, 256)
        x = jax.random.normal(k1, (B, L, Dm), dtype=jnp.float32)
        w_qkv = jax.random.normal(k2, (Dm, 3 * Dm), dtype=jnp.float32) * (1.0 / math.sqrt(Dm))
        b_qkv = jnp.zeros((3 * Dm,), dtype=jnp.float32)
        w_out = jax.random.normal(k3, (Dm, Dm), dtype=jnp.float32) * (1.0 / math.sqrt(Dm))
        b_out = jnp.zeros((Dm,), dtype=jnp.float32)
        return {'x': x, 'w_qkv': w_qkv, 'b_qkv': b_qkv, 'w_out': w_out, 'b_out': b_out}
    _L0_attn_in = _L0_attn_setup()

    def _L0_ffn_setup():
        import jax, jax.numpy as jnp
        import numpy as np
        B, S, D, T = (4, 1024, 256, 8)
        key = jax.random.key(seed)
        k1, k2, k3, k4 = jax.random.split(key, 4)
        x = jax.random.normal(k1, (B, S, D), dtype=jnp.float32)
        tile_sigs = jax.random.normal(k2, (T, D), dtype=jnp.float32)
        bound = 1.0 / np.sqrt(D)
        W = jax.random.uniform(k3, (T, D, D), minval=-bound, maxval=bound, dtype=jnp.float32)
        b = jax.random.uniform(k4, (T, D), minval=-bound, maxval=bound, dtype=jnp.float32)
        return {'x': x, 'tile_sigs': tile_sigs, 'W': W, 'b': b}
    _L0_ffn_in = _L0_ffn_setup()
    _d = {'L0_attn_x': _L0_attn_in['x'], 'L0_attn_w_qkv': _L0_attn_in['w_qkv'], 'L0_attn_b_qkv': _L0_attn_in['b_qkv'], 'L0_attn_w_out': _L0_attn_in['w_out'], 'L0_attn_b_out': _L0_attn_in['b_out'], 'L0_ffn_tile_sigs': _L0_ffn_in['tile_sigs'], 'L0_ffn_W': _L0_ffn_in['W'], 'L0_ffn_b': _L0_ffn_in['b']}
    _x0 = _d['L0_attn_x']
    _d['L0_attn_x'] = jax.random.normal(jax.random.fold_in(jax.random.key(seed), 1), (2, 2048, 256), dtype=_x0.dtype)
    del _x0
    return _d

def reference(L0_attn_x, L0_attn_w_qkv, L0_attn_b_qkv, L0_attn_w_out, L0_attn_b_out, L0_ffn_tile_sigs, L0_ffn_W, L0_ffn_b):

    def _L0_attn_ref(x, w_qkv, b_qkv, w_out, b_out):
        import jax, jax.numpy as jnp
        import numpy as np
        import math
        THETA = 500.0
        SCALE = 1.0
        NUM_HEADS = 16

        def apply_rope(t, theta=THETA, scale=SCALE):
            D = t.shape[-1]
            L = t.shape[-2]
            half = D // 2
            freqs = 1.0 / theta ** (jnp.arange(half, dtype=jnp.float32) / half)
            angles = scale * jnp.arange(L, dtype=jnp.float32)[:, None] * freqs[None, :]
            cos = jnp.cos(angles)
            sin = jnp.sin(angles)
            t1, t2 = (t[..., :half], t[..., half:])
            return jnp.concatenate([t1 * cos - t2 * sin, t1 * sin + t2 * cos], axis=-1)
        B, L, Dm = x.shape
        H = NUM_HEADS
        Dh = Dm // H
        qkv = x @ w_qkv + b_qkv
        qkv = qkv.reshape(B, L, 3, H, Dh)
        qkv = jnp.swapaxes(qkv, 1, 3)
        q, k, v = (qkv[:, :, 0], qkv[:, :, 1], qkv[:, :, 2])
        q = apply_rope(q)
        k = apply_rope(k)
        scale = 1.0 / math.sqrt(Dh)
        w = jnp.einsum('bhqd,bhkd->bhqk', q, k * scale)
        w = jax.nn.softmax(w, axis=-1)
        o = jnp.einsum('bhqk,bhkd->bhqd', w, v)
        o = jnp.swapaxes(o, 1, 2).reshape(B, L, H * Dh)
        return o @ w_out + b_out

    def _L0_ffn_ref(x, tile_sigs, W, b):
        import jax, jax.numpy as jnp
        import numpy as np
        B, S, D, T = (4, 1024, 256, 8)
        scores = jnp.einsum('bsd,td->bst', x, jnp.sign(tile_sigs))
        idx = jnp.argmax(scores, axis=-1)
        all_out = jnp.einsum('bsd,tde->bste', x, W) + b[None, None]
        out = jnp.take_along_axis(all_out, idx[:, :, None, None], axis=2)
        return out[:, :, 0, :]
    x = L0_attn_x
    xn = _layernorm(x, axis=-1)
    x = x + _L0_attn_ref(xn, L0_attn_w_qkv, L0_attn_b_qkv, L0_attn_w_out, L0_attn_b_out) + _L0_ffn_ref(xn, L0_ffn_tile_sigs, L0_ffn_W, L0_ffn_b)
    return x

_drawn_inputs = setup_inputs


def setup_inputs(seed=0):
    import zlib

    import numpy as np

    out = dict(_drawn_inputs(seed))
    spreads = {'L0_attn_b_qkv': (0.0, 0.1), 'L0_attn_b_out': (0.0, 0.1)}
    factors = {}
    for name, (base, spread) in spreads.items():
        noise = np.random.default_rng([zlib.crc32(name.encode()), seed]).standard_normal(out[name].shape)
        drawn = base * np.exp(spread * noise) if base else spread * noise
        out[name] = jnp.asarray(drawn.astype(out[name].dtype))
    for name, factor in factors.items():
        out[name] = (out[name] * factor).astype(out[name].dtype)
    return out
```

```python
from contextlib import ExitStack

import numpy as np

import concourse.bass as bass
from concourse import mybir

ALU = mybir.AluOpType
ACT = mybir.ActivationFunctionType
F32 = mybir.dt.float32
BF16 = mybir.dt.bfloat16
AX_X = mybir.AxisListType.X

P = 128
B, L, D = 2, 2048, 256
H = 16
DH = D // H
T = 8
THETA = 500.0
EPS = 1e-5

TOKENS = B * L
TILES = TOKENS // P
KD = D // P
GROUP = 512
GT = GROUP // P
GROUPS = L // GROUP
MB = 2 * KD
PARTS = 3

SLOTS = B * H
KT = L // P
QC = L // 512
HEAD_BUFS = 4
P_BUFS = 2
RS = 6 * DH
PAIRS = ((0, 0), (0, 1), (0, 2), (1, 0), (1, 1), (2, 0))
RA = RS + PARTS
VW = 32


def build_tables():
    half = DH // 2
    freqs = (1.0 / np.float32(THETA) ** (np.arange(half, dtype=np.float32) / np.float32(half))).astype(np.float32)
    angles = np.arange(L, dtype=np.float32)[None, :] * freqs[:, None]
    cos, sin = np.cos(angles), np.sin(angles)
    rope = np.stack([np.concatenate([cos, cos]), np.concatenate([-sin, sin])]).astype(np.float32)
    ident = np.eye(P, dtype=np.float32)
    swap = np.zeros((P, P), np.float32)
    for m in range(P):
        head, d = divmod(m, DH)
        swap[head * DH + (d + half) % DH, m] = 1.0
    pick = np.zeros((P, QC, DH + 1), np.float32)
    for c in range(QC):
        for d in range(DH + 1):
            pick[VW * c + d, c, d] = 1.0
    rank = np.arange(T, 0, -1, dtype=np.float32)[None, :]
    return rope, ident, swap, pick.reshape(P, -1), rank


def routed_attention_kernel(nc, x, w_qkv, b_qkv, w_out, b_out, sigs_t, ffn_w, ffn_b,
                            bqk_cols, rope, ident, swap, pick, rank, out):
    parts_dram = nc.dram_tensor("qk_parts", (PARTS, 2 * D, TOKENS), BF16, kind="Internal").ap()
    xt_dram = nc.dram_tensor("xn_transposed", (TILES, P, KD, P), F32, kind="Internal").ap()
    bp_dram = nc.dram_tensor("ffn_bias_parts", (PARTS, T * D), BF16, kind="Internal").ap()

    with ExitStack() as top:
        def keep(name, shape, dt=F32):
            return top.enter_context(nc.sbuf_tensor(name, shape, dt))

        v_sb = keep("v_sb", [P, TILES, D])
        ffnw_sb = keep("ffnw_sb", [P, KD, T * D])
        onehot = keep("onehot", [P, TILES, T])
        ident_sb = keep("ident_sb", [P, P])
        pick_sb = keep("pick_sb", [P, QC * (DH + 1)])
        wout_sb = keep("wout_sb", [P, KD, D])
        bout_row = keep("bout_row", [P, D])
        bias3 = keep("bias3", [P, T * D], BF16)
        ones3 = keep("ones3", [P, P], BF16)
        ident_bf = keep("ident_bf", [P, P], BF16)

        stage_a(nc, x, w_qkv, b_qkv, w_out, b_out, sigs_t, ffn_w, ffn_b, bqk_cols, rope, ident, swap, pick, rank,
                parts_dram, xt_dram, bp_dram, v_sb, ffnw_sb, onehot, ident_sb, ident_bf, pick_sb, wout_sb,
                bout_row, bias3, ones3)
        ffn_sb = keep("ffn_sb", [P, TILES, D])
        o_sb = keep("o_sb", [P, SLOTS, KT, DH])
        stage_b(nc, parts_dram, xt_dram, v_sb, ffn_sb, o_sb, ffnw_sb, onehot, ident_bf, pick_sb, bias3, ones3)
        stage_c(nc, x, out, o_sb, ffn_sb, ident_sb, wout_sb, bout_row)


def stage_a(nc, x, w_qkv, b_qkv, w_out, b_out, sigs_t, ffn_w, ffn_b, bqk_cols, rope, ident, swap, pick, rank,
            parts_dram, xt_dram, bp_dram, v_sb, ffnw_sb, onehot, ident_sb, ident_bf, pick_sb, wout_sb,
            bout_row, bias3, ones3):
    UNITS = GROUPS * MB
    VN = D + T
    with ExitStack() as ctx:
        def sb(name, shape, dt=F32):
            return ctx.enter_context(nc.sbuf_tensor(name, shape, dt))

        def sem(name):
            return ctx.enter_context(nc.semaphore(name))

        wqk_sb = sb("wqk_sb", [P, KD, 2 * D])
        wvs_sb = sb("wvs_sb", [P, KD, VN])
        sig_sb = sb("sig_sb", [P, KD, T])
        sneg = sb("sneg", [P, KD, T])
        spos = sb("spos", [P, KD, T])
        swap_sb = sb("swap_sb", [P, P])
        cos_sb = sb("cos_sb", [P, L])
        sin_sb = sb("sin_sb", [P, L])
        bqk_raw = sb("bqk_raw", [P, MB])
        bqk = sb("bqk", [P, MB])
        bv_row = sb("bv_row", [P, D])
        rank_row = sb("rank_row", [P, T])
        eps_col = sb("eps_col", [P, 1])
        x_sb = [sb(f"x_sb{i}", [P, GT, D]) for i in range(2)]
        xn_sb = [sb(f"xn_sb{i}", [P, GT, D]) for i in range(2)]
        xt_sb = [sb(f"xt_sb{i}", [P, KD, GROUP]) for i in range(2)]
        stats = sb("stats", [P, GT, 6])
        count_seen = sb("count_seen", [P, 1])
        moments = sb("moments", [P, GT, 2])
        std = sb("std", [P, GT])
        rstd = sb("rstd", [P, GT])
        gate = sb("gate", [P, GT, T])
        gmax = sb("gmax", [P, GT])
        ranked = sb("ranked", [P, GT, T])
        first = sb("first", [P, GT])
        qk_sb = [sb(f"qk_sb{i}", [P, GROUP]) for i in range(2)]
        qcos = [sb(f"qcos{i}", [P, GROUP]) for i in range(2)]
        qsin = [sb(f"qsin{i}", [P, GROUP]) for i in range(2)]
        roped = [sb(f"roped{i}", [P, GROUP]) for i in range(2)]
        rest = [sb(f"rest{i}", [P, GROUP]) for i in range(4)]
        fb_sb = sb("fb_sb", [P, T * D // P])
        fb_rest = sb("fb_rest", [P, 2, T * D // P])
        fb_parts = sb("fb_parts", [P, PARTS, T * D // P], BF16)
        parts = [sb(f"parts{i}", [P, PARTS, MB, GROUP], BF16) for i in range(2)]

        xt_ps = [ctx.enter_context(nc.psum_tensor(f"xt_ps{k}", [P, GROUP], F32)) for k in range(KD)]
        qk_ps = [ctx.enter_context(nc.psum_tensor(f"qk_ps{k}", [P, GROUP], F32)) for k in range(2)]
        sw_ps = [ctx.enter_context(nc.psum_tensor(f"sw_ps{k}", [P, GROUP], F32)) for k in range(2)]
        v_ps = [ctx.enter_context(nc.psum_tensor(f"v_ps{k}", [P, 512], F32)) for k in range(2)]

        weights_in = sem("weights_in")
        late_in = sem("late_in")
        x_in = [sem(f"x_in{i}") for i in range(2)]
        consts_done = sem("consts_done")
        signs_done = sem("signs_done")
        bparts_done = sem("bparts_done")
        bparts_out = sem("bparts_out")
        stats_done = sem("stats_done")
        moments_done = sem("moments_done")
        std_done = sem("std_done")
        rstd_done = sem("rstd_done")
        xn_done = sem("xn_done")
        xt_mm = sem("xt_mm")
        xt_done = sem("xt_done")
        xt_out = [sem(f"xt_out{i}") for i in range(2)]
        qk_mm = sem("qk_mm")
        qk_done = sem("qk_done")
        v_mm = sem("v_mm")
        v_done = sem("v_done")
        gate_step = sem("gate_step")
        swap_mm = sem("swap_mm")
        qcos_done = sem("qcos_done")
        qsin_done = sem("qsin_done")
        roped_done = sem("roped_done")
        hi_done = sem("hi_done")
        rest_done = sem("rest_done")
        mid_done = sem("mid_done")
        lo_done = sem("lo_done")
        parts_out = [sem(f"parts_out{i}") for i in range(2)]

        x_view = x.rearrange("b (g t p) d -> b g p t d", t=GT, p=P)
        xt_view = xt_dram.rearrange("(n t) p k q -> n p k t q", t=GT)
        gp_consts = sem("gp_consts")
        N_WEIGHTS = 9 + 2 * (P // DH)
        block = ctx.enter_context(nc.Block())


        @block.sync
        def _(sp):
            def load_x(b, g):
                sp.wait_ge(xn_done, b * GROUPS + g + 1)
                sp.dma_start(x_sb[g % 2][:], x_view[bass.ds(b, 1), g].rearrange("a p t d -> (a p) t d")).then_inc(x_in[g % 2], 16)

            def const(to, of, signal):
                sp.dma_start(to, of).then_inc(signal, 16)

            for i in range(2):
                sp.sem_inc(xt_out[i], 16)
                sp.sem_inc(parts_out[i], 16)
            const(ident_sb[:], ident, weights_in)
            const(wqk_sb[:], w_qkv[:, 0:2 * D].rearrange("(k p) n -> p k n", p=P), weights_in)
            const(bqk_raw[:], bqk_cols, weights_in)
            const(wvs_sb[:, :, 0:D], w_qkv[:, 2 * D:3 * D].rearrange("(k p) n -> p k n", p=P), weights_in)
            const(sig_sb[:], sigs_t.rearrange("(k p) t -> p k t", p=P), weights_in)
            const(swap_sb[:], swap, weights_in)
            const(bv_row[:], b_qkv[2 * D:3 * D].partition_broadcast(P), weights_in)
            const(rank_row[:], rank[0, :].partition_broadcast(P), weights_in)
            const(fb_sb[:], ffn_b.rearrange("t d -> (t d)").rearrange("(p n) -> p n", p=P), weights_in)
            for n, table in enumerate((cos_sb, sin_sb)):
                for h in range(P // DH):
                    const(table[h * DH:(h + 1) * DH, :], rope[n], weights_in)
            with sp.Fori(0, B) as b:
                load_x(b, 0)
                load_x(b, 1)
                for g in range(GROUPS):
                    G = b * GROUPS + g
                    if g + 2 < GROUPS:
                        load_x(b, g + 2)
                    sp.wait_ge(xt_done, G + 2)
                    for k in range(KD):
                        sp.dma_start(xt_view[bass.ds(G, 1), :, k].rearrange("n p t q -> (n p) t q"),
                                     xt_sb[g % 2][:, k, :].rearrange("p (t q) -> p t q", q=P)).then_inc(xt_out[g % 2], 16)
                    sp.wait_ge(lo_done, (G + 1) * MB + 4)
                    for a in range(PARTS):
                        sp.dma_start(parts_dram[a].rearrange("(m p) n -> p m n", p=P)[:, :, bass.ds(G * GROUP, GROUP)],
                                     parts[g % 2][:, a]).then_inc(parts_out[g % 2], 16)
            for k in range(KD):
                const(ffnw_sb[:, k].rearrange("p (t n) -> p t n", t=T), ffn_w[:, k * P:(k + 1) * P, :].rearrange("t p n -> p t n"), late_in)
            const(wout_sb[:], w_out.rearrange("(k p) n -> p k n", p=P), late_in)
            const(pick_sb[:], pick, late_in)
            const(bout_row[:], b_out.partition_broadcast(P), late_in)
            sp.wait_ge(bparts_done, 5)
            for a in range(PARTS):
                sp.dma_start(bp_dram[a].rearrange("(p n) -> p n", p=P), fb_parts[:, a]).then_inc(bparts_out, 16)
            sp.wait_ge(bparts_out, 16 * PARTS)
            const(bias3[0:PARTS, :], bp_dram, late_in)
            sp.wait_ge(late_in, 16 * (KD + 4))
            for i in range(2):
                sp.wait_ge(xt_out[i], 16 * (1 + KD * B * GROUPS // 2))
                sp.wait_ge(parts_out[i], 16 * (1 + PARTS * B * GROUPS // 2))

        @block.scalar
        def _(act):
            act.sem_inc(xt_done, 1)
            act.sem_inc(qk_done, 2)
            act.wait_ge(consts_done, 3)
            with act.Fori(0, B) as b:
                def std_dev(g):
                    act.wait_ge(moments_done, b * GROUPS + g + 1)
                    nc.scalar.activation(std[:], moments[:, :, 1], ACT.Sqrt, bias=eps_col[:]).then_inc(std_done, 1)

                def copy_xt(g):
                    G = b * GROUPS + g
                    act.wait_ge(xt_mm, G + 3)
                    act.wait_ge(v_mm, G * GT + 4)
                    act.wait_ge(xt_out[g % 2], (b * (GROUPS // 2) + g // 2) * 16 * KD + 16)
                    for k in range(KD):
                        last = nc.scalar.copy(xt_sb[g % 2][:, k, :], xt_ps[k][:])
                    last.then_inc(xt_done, 1)

                def add_bias(s):
                    n, m = b * UNITS + s, s % MB
                    act.wait_ge(qk_mm, n + 1)
                    act.wait_ge(swap_mm, n + 1)
                    act.wait_ge(qcos_done, n + 1)
                    nc.scalar.activation(qk_sb[s % 2][:], qk_ps[s % 2][:], ACT.Identity, bias=bqk[:, m:m + 1],
                                         scale=1.0 if m < KD else float(DH) ** -0.5).then_inc(qk_done, 1)

                def hi_part(s):
                    g, m = divmod(s, MB)
                    act.wait_ge(roped_done, b * UNITS + s + 3)
                    if m == 0:
                        act.wait_ge(parts_out[g % 2], (b * (GROUPS // 2) + g // 2) * 16 * PARTS + 16)
                    nc.scalar.copy(parts[g % 2][:, 0, m, :], roped[s % 2][:]).then_inc(hi_done, 1)

                def mid_part(s):
                    g, m = divmod(s, MB)
                    act.wait_ge(rest_done, b * UNITS + s + 3)
                    nc.scalar.copy(parts[g % 2][:, 1, m, :], rest[s % 4][:]).then_inc(mid_done, 1)

                std_dev(0)
                copy_xt(0)
                for s in range(UNITS + 3):
                    g, m = divmod(s, MB)
                    if m == 1 and g + 1 < GROUPS:
                        std_dev(g + 1)
                    if s < UNITS:
                        add_bias(s)
                    if 2 <= s < UNITS + 2:
                        hi_part(s - 2)
                    if 3 <= s:
                        mid_part(s - 3)
                    if m == 3 and g + 1 < GROUPS:
                        copy_xt(g + 1)

        @block.gpsimd
        def _(pool):
            pool.sem_inc(qcos_done, 2)
            pool.sem_inc(rest_done, 2)
            pool.memset(bias3[:], 0.0).then_inc(gp_consts, 1)
            pool.memset(ones3[:], 1.0).then_inc(gp_consts, 1)
            pool.wait_ge(weights_in, 16 * N_WEIGHTS)
            with pool.Fori(0, B) as b:
                for s in range(UNITS + 2):
                    if s < UNITS:
                        n, g = b * UNITS + s, s // MB
                        pool.wait_ge(qk_done, n + 3)
                        pool.wait_ge(roped_done, n + 1)
                        nc.gpsimd.tensor_tensor(qcos[s % 2][:], qk_sb[s % 2][:], cos_sb[:, g * GROUP:(g + 1) * GROUP],
                                                ALU.mult).then_inc(qcos_done, 1)
                    if s >= 2:
                        n, g, m = b * UNITS + s - 2, (s - 2) // MB, (s - 2) % MB
                        pool.wait_ge(hi_done, n + 1)
                        pool.wait_ge(lo_done, n + 1)
                        nc.gpsimd.tensor_tensor(rest[(s - 2) % 4][:], roped[s % 2][:], parts[g % 2][:, 0, m, :],
                                                ALU.subtract).then_inc(rest_done, 1)

        @block.vector
        def _(dve):
            dve.sem_inc(xn_done, 2)
            dve.sem_inc(roped_done, 2)
            dve.sem_inc(qsin_done, 2)
            dve.sem_inc(lo_done, 4)
            dve.sem_inc(v_done, 2)
            dve.memset(eps_col[:], EPS).then_inc(consts_done, 1)
            dve.wait_ge(weights_in, 16 * N_WEIGHTS)
            nc.vector.tensor_scalar(spos[:], sig_sb[:], 0.0, None, ALU.is_gt).then_inc(signs_done, 1)
            nc.vector.tensor_scalar(sneg[:], sig_sb[:], 0.0, None, ALU.is_lt).then_inc(signs_done, 1)
            dve.wait_ge(signs_done, 2)
            nc.vector.tensor_tensor(wvs_sb[:, :, D:VN], spos[:], sneg[:], ALU.subtract).then_inc(signs_done, 1)
            nc.vector.tensor_copy(bqk[:, 0:KD], bqk_raw[:, 0:KD]).then_inc(consts_done, 1)
            nc.vector.tensor_scalar(bqk[:, KD:MB], bqk_raw[:, KD:MB], float(DH) ** -0.5, None, ALU.mult).then_inc(consts_done, 1)
            nc.vector.tensor_copy(ident_bf[:], ident_sb[:]).then_inc(consts_done, 1)
            nc.vector.tensor_copy(fb_parts[:, 0], fb_sb[:]).then_inc(bparts_done, 1)
            dve.wait_ge(bparts_done, 1)
            nc.vector.tensor_tensor(fb_rest[:, 0], fb_sb[:], fb_parts[:, 0], ALU.subtract).then_inc(bparts_done, 1)
            dve.wait_ge(bparts_done, 2)
            nc.vector.tensor_copy(fb_parts[:, 1], fb_rest[:, 0]).then_inc(bparts_done, 1)
            dve.wait_ge(bparts_done, 3)
            nc.vector.tensor_tensor(fb_rest[:, 1], fb_rest[:, 0], fb_parts[:, 1], ALU.subtract).then_inc(bparts_done, 1)
            dve.wait_ge(bparts_done, 4)
            nc.vector.tensor_copy(fb_parts[:, 2], fb_rest[:, 1]).then_inc(bparts_done, 1)

            with dve.Fori(0, B) as b:
                def norm(g):
                    G = b * GROUPS + g
                    dve.wait_ge(x_in[g % 2], (b * (GROUPS // 2) + g // 2) * 16 + 16)
                    for t in range(GT):
                        last = nc.vector.bn_stats(stats[:, t, :], x_sb[g % 2][:, t, :])
                    last.then_inc(stats_done, 1)
                    dve.wait_ge(stats_done, G + 1)
                    nc.vector.tensor_copy(count_seen[:], stats[:, 0, 0:1])
                    for t in range(GT):
                        last = nc.vector.bn_aggr(moments[:, t, :], stats[:, t, :])
                    last.then_inc(moments_done, 1)
                    dve.wait_ge(std_done, G + 1)
                    nc.vector.reciprocal(rstd[:], std[:]).then_inc(rstd_done, 1)
                    dve.wait_ge(rstd_done, G + 1)
                    dve.wait_ge(xt_mm, G + 1)
                    for t in range(GT):
                        last = nc.vector.tensor_scalar(xn_sb[g % 2][:, t, :], x_sb[g % 2][:, t, :], moments[:, t, 0:1],
                                                       rstd[:, t:t + 1], ALU.subtract, ALU.mult)
                    last.then_inc(xn_done, 1)

                def take_v(s):
                    n, t = b * GROUPS * GT + s, s % GT
                    dve.wait_ge(v_mm, n + 1 + 8)
                    nc.vector.tensor_tensor(v_sb[:, bass.ds(n, 1), :].rearrange("p a d -> p (a d)"), v_ps[s % 2][:, 0:D],
                                            bv_row[:], ALU.add)
                    nc.vector.tensor_copy(gate[:, t, :], v_ps[s % 2][:, D:VN]).then_inc(v_done, 1)

                def route(g):
                    G = b * GROUPS + g
                    dve.wait_ge(v_done, (G + 1) * GT + 2)
                    nc.vector.tensor_reduce(gmax[:], gate[:], AX_X, ALU.max).then_inc(gate_step, 1)
                    dve.wait_ge(gate_step, G * 4 + 1)
                    for t in range(GT):
                        last = nc.vector.scalar_tensor_tensor(ranked[:, t, :], gate[:, t, :], gmax[:, t:t + 1], rank_row[:],
                                                              ALU.is_equal, ALU.mult)
                    last.then_inc(gate_step, 1)
                    dve.wait_ge(gate_step, G * 4 + 2)
                    nc.vector.tensor_reduce(first[:], ranked[:], AX_X, ALU.max).then_inc(gate_step, 1)
                    dve.wait_ge(gate_step, G * 4 + 3)
                    for t in range(GT):
                        last = nc.vector.tensor_scalar(onehot[:, bass.ds(G * GT + t, 1), :].rearrange("p a e -> p (a e)"),
                                                       rank_row[:], first[:, t:t + 1], None, ALU.is_equal)
                    last.then_inc(gate_step, 1)

                def rope_sum(s):
                    n, g = b * UNITS + s, s // MB
                    dve.wait_ge(swap_mm, n + 3)
                    dve.wait_ge(roped_done, n + 1)
                    nc.vector.tensor_tensor(qsin[s % 2][:], sw_ps[s % 2][:], sin_sb[:, g * GROUP:(g + 1) * GROUP],
                                            ALU.mult).then_inc(qsin_done, 1)
                    dve.wait_ge(qcos_done, n + 3)
                    dve.wait_ge(qsin_done, n + 3)
                    dve.wait_ge(rest_done, n + 1)
                    nc.vector.tensor_tensor(roped[s % 2][:], qcos[s % 2][:], qsin[s % 2][:], ALU.add).then_inc(roped_done, 1)

                def lo_part(s):
                    n, g, m = b * UNITS + s, s // MB, s % MB
                    dve.wait_ge(rest_done, n + 3)
                    dve.wait_ge(mid_done, n + 1)
                    nc.vector.tensor_tensor(parts[g % 2][:, 2, m, :], rest[s % 4][:], parts[g % 2][:, 1, m, :],
                                            ALU.subtract).then_inc(lo_done, 1)

                norm(0)
                for s in range(1, UNITS + 4):
                    if s % MB == 1 and s > MB:
                        route(s // MB - 1)
                    if s <= UNITS:
                        take_v(s - 1)
                        rope_sum(s - 1)
                    if 4 <= s < UNITS + 4:
                        lo_part(s - 4)
                    if s % MB == 1 and s // MB + 1 < GROUPS:
                        norm(s // MB + 1)

        @block.tensor
        def _(pe):
            pe.sem_inc(xt_mm, 2)
            pe.sem_inc(swap_mm, 2)
            pe.sem_inc(v_mm, 8)
            pe.wait_ge(weights_in, 16 * N_WEIGHTS)
            pe.wait_ge(signs_done, 3)
            with pe.Fori(0, B) as b:
                def transposes(g):
                    G = b * GROUPS + g
                    pe.wait_ge(xn_done, G + 3)
                    pe.wait_ge(xt_done, G + 1)
                    for k in range(KD):
                        for t in range(GT):
                            last = nc.tensor.transpose(xt_ps[k][:, t * P:(t + 1) * P], xn_sb[g % 2][:, t, k * P:(k + 1) * P],
                                                       ident_sb[:])
                    last.then_inc(xt_mm, 1)

                def project(s):
                    g, m = divmod(s, MB)
                    if m == 0:
                        pe.wait_ge(xt_done, b * GROUPS + g + 2)
                    pe.wait_ge(qk_done, b * UNITS + s + 1)
                    for k in range(KD):
                        last = nc.tensor.matmul(qk_ps[s % 2][:], wqk_sb[:, k, m * P:(m + 1) * P], xt_sb[g % 2][:, k, :],
                                                start=(k == 0), stop=(k == KD - 1))
                    last.then_inc(qk_mm, 1)

                def project_v(s):
                    g, t = divmod(s, GT)
                    pe.wait_ge(v_done, b * GROUPS * GT + s + 1)
                    for k in range(KD):
                        last = nc.tensor.matmul(v_ps[s % 2][:, 0:VN], xt_sb[g % 2][:, k, t * P:(t + 1) * P], wvs_sb[:, k, :],
                                                start=(k == 0), stop=(k == KD - 1))
                    last.then_inc(v_mm, 1)

                def swap_halves(s):
                    pe.wait_ge(qk_done, b * UNITS + s + 3)
                    pe.wait_ge(qsin_done, b * UNITS + s + 1)
                    nc.tensor.matmul(sw_ps[s % 2][:], swap_sb[:], qk_sb[s % 2][:], start=True, stop=True).then_inc(swap_mm, 1)

                transposes(0)
                for s in range(UNITS + 1):
                    if s < UNITS:
                        project(s)
                    if s >= 1:
                        project_v(s - 1)
                        swap_halves(s - 1)
                    if s % MB == MB - 1 and s // MB + 1 < GROUPS:
                        transposes(s // MB + 1)


def stage_b(nc, parts_dram, xt_dram, v_sb, ffn_sb, o_sb, ffnw_sb, onehot, ident_bf, pick_sb, bias3, ones3):
    PICK = DH + 1
    SHIFT = PARTS * KT
    LOADS = 13
    MAX_USES = KT * QC
    FFN_USES = T * D // 512
    USES = MAX_USES + FFN_USES
    with ExitStack() as ctx:
        def sb(name, shape, dt=F32):
            return ctx.enter_context(nc.sbuf_tensor(name, shape, dt))

        def psum(name, shape):
            return ctx.enter_context(nc.psum_tensor(name, shape, F32))

        def sem(name):
            return ctx.enter_context(nc.semaphore(name))

        q_st = [sb(f"q_st{i}", [P, L], BF16) for i in range(HEAD_BUFS)]
        k_st = [sb(f"k_st{i}", [P, L], BF16) for i in range(HEAD_BUFS)]
        vh = [sb(f"vh{i}", [P, KT, VW]) for i in range(HEAD_BUFS)]
        xt = [sb(f"xt{i}", [P, KD, P]) for i in range(HEAD_BUFS)]
        probs = [sb(f"probs{i}", [P, L]) for i in range(P_BUFS)]
        chunk_max = sb("chunk_max", [P, KT, QC])
        neg_max = sb("neg_max", [P, KT])
        shift = sb("shift", [P, P], BF16)
        shift_rest = sb("shift_rest", [P, 2, KT])
        shift_rows = sb("shift_rows", [SHIFT, P], BF16)
        o_acc = sb("o_acc", [P, 512])
        rden = sb("rden", [P, KT])

        st_ps = [psum(f"st_ps{i}", [P, L // 2]) for i in range(2)]
        wide_ps = [psum(f"wide_ps{i}", [P, 512]) for i in range(2)]
        o_ps = psum("o_ps", [P, 512])
        turn_ps = psum("turn_ps", [P, 512])

        stack_in = [sem(f"stack_in{i}") for i in range(HEAD_BUFS)]
        consts_done = sem("b_consts_done")
        vh_done = sem("vh_done")
        shift_in = sem("shift_in")
        shift_zeroed = sem("shift_zeroed")
        st_mm = sem("st_mm")
        exp_done = sem("exp_done")
        pv_mm = sem("pv_mm")
        o_read = sem("o_read")
        o_turned = sem("o_turned")
        o_done = sem("o_done")
        wide_mm = sem("wide_mm")
        wide_read = sem("wide_read")
        max_done = sem("max_done")
        shift_step = sem("shift_step")
        shift_turned = sem("shift_turned")
        shift_read = sem("shift_read")
        ffn_step = sem("ffn_step")
        rden_done = sem("rden_done")
        block = ctx.enter_context(nc.Block())

        BODIES = SLOTS // HEAD_BUFS

        @block.sync
        def _(sp):
            with sp.Fori(0, B) as b:
                with sp.Fori(0, H // HEAD_BUFS) as j:
                    for u in range(HEAD_BUFS):
                        slot = b * H + j * HEAD_BUFS + u
                        sp.wait_ge(o_read, slot + 2)
                        cols = bass.ds(b * L, L)
                        row = (j * HEAD_BUFS + u) * DH

                        def stack(to, r, a, first):
                            sp.dma_start(to[r * DH:(r + 1) * DH, :], parts_dram[a, bass.ds(row + first, DH), cols]).then_inc(stack_in[u], 16)

                        for r, (qa, ka) in enumerate(PAIRS):
                            stack(q_st[u], r, qa, 0)
                            stack(k_st[u], r, ka, D)
                        sp.dma_start(xt[u][:], xt_dram[bass.ds(slot, 1)].rearrange("n p k q -> (n p) k q")).then_inc(stack_in[u], 16)

        @block.gpsimd
        def _(pool):
            for i in range(HEAD_BUFS):
                pool.memset(vh[i][:], 0.0).then_inc(consts_done, 1)
            pool.wait_ge(consts_done, HEAD_BUFS)
            for i in range(HEAD_BUFS):
                pool.memset(vh[i][:, :, DH:DH + 1], 1.0).then_inc(consts_done, 1)
            pool.wait_ge(consts_done, 2 * HEAD_BUFS)
            with pool.Fori(0, B) as b:
                with pool.Fori(0, H // HEAD_BUFS) as j:
                    for u in range(HEAD_BUFS):
                        pool.wait_ge(o_read, b * H + j * HEAD_BUFS + u + 1)
                        nc.gpsimd.tensor_copy(vh[u][:, :, 0:DH], v_sb[:, bass.ds(b * KT, KT), bass.ds((j * HEAD_BUFS + u) * DH, DH)]).then_inc(vh_done, 1)

        @block.scalar
        def _(act):
            act.sem_inc(exp_done, 2)
            act.sem_inc(o_read, HEAD_BUFS)

            def load_shift(slot, u):
                act.wait_ge(shift_read, slot + 1)
                for a in range(PARTS):
                    act.dma_start(q_st[u][RS + a:RS + a + 1, :].rearrange("a (t q) -> a t q", q=P),
                                  shift_rows[a * KT:(a + 1) * KT, :]).then_inc(shift_in, 16)

            def slot_work(slot, u, last):
                for kt in range(KT):
                    act.wait_ge(pv_mm, slot * KT + kt + 1)
                    for half in range(2):
                        act.wait_ge(st_mm, slot * 2 * KT + 2 * kt + half + 1)
                        nc.scalar.activation(probs[kt % 2][:, half * (L // 2):(half + 1) * (L // 2)], st_ps[half][:],
                                             ACT.Exp).then_inc(exp_done, 1)
                act.wait_ge(pv_mm, slot * KT + KT + P_BUFS)
                act.wait_ge(o_turned, slot + 1)
                nc.scalar.copy(o_acc[:], o_ps[:]).then_inc(o_read, 1)
                if not last:
                    load_shift(slot + 1, (u + 1) % HEAD_BUFS)

            load_shift(0, 0)
            with act.Fori(0, BODIES - 1) as i:
                for u in range(HEAD_BUFS):
                    slot_work(i * HEAD_BUFS + u, u, False)
            for u in range(HEAD_BUFS):
                slot_work(SLOTS - HEAD_BUFS + u, u, u == HEAD_BUFS - 1)

        @block.vector
        def _(dve):
            dve.memset(shift[:], 0.0).then_inc(shift_zeroed, 1)
            for i in range(HEAD_BUFS):
                dve.memset(k_st[i][RS:RA, :], 1.0).then_inc(shift_zeroed, 1)
            dve.wait_ge(shift_zeroed, 1 + HEAD_BUFS)
            dve.sem_inc(wide_read, 2)
            dve.sem_inc(o_done, 1)

            def take_max(use, kt, j):
                dve.wait_ge(wide_mm, use + 1)
                nc.vector.tensor_reduce(chunk_max[:, kt, j:j + 1], wide_ps[j % 2][:], AX_X, ALU.max).then_inc(wide_read, 1)

            def make_shift(slot, use):
                dve.wait_ge(wide_read, use + 2)
                nc.vector.tensor_reduce(neg_max[:], chunk_max[:], AX_X, ALU.max, negate=True).then_inc(max_done, 1)
                dve.wait_ge(max_done, slot + 1)
                nc.vector.tensor_copy(shift[:, 0 * KT:1 * KT], neg_max[:]).then_inc(shift_step, 1)
                dve.wait_ge(shift_step, slot * 5 + 1)
                nc.vector.tensor_tensor(shift_rest[:, 0, :], neg_max[:], shift[:, 0 * KT:1 * KT], ALU.subtract).then_inc(shift_step, 1)
                dve.wait_ge(shift_step, slot * 5 + 2)
                nc.vector.tensor_copy(shift[:, 1 * KT:2 * KT], shift_rest[:, 0, :]).then_inc(shift_step, 1)
                dve.wait_ge(shift_step, slot * 5 + 3)
                nc.vector.tensor_tensor(shift_rest[:, 1, :], shift_rest[:, 0, :], shift[:, 1 * KT:2 * KT], ALU.subtract).then_inc(shift_step, 1)
                dve.wait_ge(shift_step, slot * 5 + 4)
                nc.vector.tensor_copy(shift[:, 2 * KT:3 * KT], shift_rest[:, 1, :]).then_inc(shift_step, 1)
                dve.wait_ge(shift_turned, slot + 1)
                nc.vector.tensor_copy(shift_rows[:], turn_ps[:].bitcast(BF16)[0:SHIFT, 0:P]).then_inc(shift_read, 1)

            def slot_work(slot, u, last):
                use = MAX_USES + slot * USES
                if not last:
                    for kt in range(KT):
                        for j in range(QC):
                            take_max(use + kt * QC + j, kt, j)
                    use = use + MAX_USES
                    dve.wait_ge(shift_in, (slot + 1) * 16 * PARTS)
                    make_shift(slot + 1, use)
                out = ffn_sb[:, bass.ds(slot, 1), :].rearrange("p a d -> p (a d)")
                for e in range(T):
                    c, half = divmod(e, 2)
                    mask = onehot[:, bass.ds(slot, 1), e:e + 1].rearrange("p a e -> p (a e)")
                    of = wide_ps[c % 2][:, half * D:(half + 1) * D]
                    if half == 0:
                        dve.wait_ge(wide_mm, use + c + 1)
                        if c > 0:
                            dve.wait_ge(wide_read, use + c + 2)
                    else:
                        dve.wait_ge(ffn_step, slot * FFN_USES + c + 1)
                    if e == 0:
                        ins = nc.vector.tensor_scalar(out, of, mask, None, ALU.mult)
                    else:
                        ins = nc.vector.scalar_tensor_tensor(out, of, mask, out, ALU.mult, ALU.add)
                    ins.then_inc(wide_read if half else ffn_step, 1)
                dve.wait_ge(o_turned, slot + 2)
                turned = turn_ps[:, 0:KT * PICK].rearrange("p (t d) -> p t d", d=PICK)
                nc.vector.reciprocal(rden[:], turned[:, :, DH]).then_inc(rden_done, 1)
                dve.wait_ge(rden_done, slot + 1)
                nc.vector.tensor_tensor(o_sb[:, bass.ds(slot, 1)].rearrange("p a t d -> p (a t) d"), turned[:, :, 0:DH],
                                        rden[:].unsqueeze(2).broadcast_to([P, KT, DH]), ALU.mult).then_inc(o_done, 1)

            for kt in range(KT):
                for j in range(QC):
                    take_max(kt * QC + j, kt, j)
            make_shift(0, MAX_USES)
            with dve.Fori(0, BODIES - 1) as i:
                for u in range(HEAD_BUFS):
                    slot_work(i * HEAD_BUFS + u, u, False)
            for u in range(HEAD_BUFS):
                slot_work(SLOTS - HEAD_BUFS + u, u, u == HEAD_BUFS - 1)

        @block.tensor
        def _(pe):
            pe.sem_inc(pv_mm, P_BUFS)
            pe.sem_inc(o_turned, 1)
            pe.wait_ge(consts_done, 2 * HEAD_BUFS)
            pe.wait_ge(shift_zeroed, 1 + HEAD_BUFS)

            def search(use, n, qt, j):
                pe.wait_ge(wide_read, use + 1)
                nc.tensor.matmul(wide_ps[j % 2][:], q_st[n][0:RS, qt * P:(qt + 1) * P], k_st[n][0:RS, j * 512:(j + 1) * 512],
                                 start=True, stop=True).then_inc(wide_mm, 1)

            def scores(slot, u, kt, half):
                pe.wait_ge(exp_done, slot * 2 * KT + 2 * kt + half + 1)
                for c in range(2):
                    q0 = half * (L // 2) + c * 512
                    last = nc.tensor.matmul(st_ps[half][:, c * 512:(c + 1) * 512], k_st[u][0:RA, kt * P:(kt + 1) * P],
                                            q_st[u][0:RA, q0:q0 + 512], start=True, stop=True)
                last.then_inc(st_mm, 1)

            def values(slot, u, kt):
                if kt == 0:
                    pe.wait_ge(o_read, slot + HEAD_BUFS)
                    pe.wait_ge(vh_done, slot + 1)
                pe.wait_ge(exp_done, slot * 2 * KT + 2 * kt + 4)
                for c in range(QC):
                    last = nc.tensor.matmul(o_ps[VW * c:VW * (c + 1), :], vh[u][:, kt, :], probs[kt % 2][:, c * 512:(c + 1) * 512],
                                            start=(kt == 0), stop=(kt == KT - 1), tile_position=(0, VW * c))
                last.then_inc(pv_mm, 1)

            def turn_shift(slot):
                pe.wait_ge(shift_step, slot * 5 + 5)
                if not isinstance(slot, int) or slot > 0:
                    pe.wait_ge(o_done, slot)
                nc.tensor.transpose(turn_ps[:].bitcast(BF16)[:, 0:P], shift[:],
                                    ident_bf[:]).then_inc(shift_turned, 1)

            def slot_work(slot, i, u, last):
                n = (u + 1) % HEAD_BUFS
                use = MAX_USES + slot * USES
                if not last:
                    pe.wait_ge(stack_in[n], (i + (u + 1) // HEAD_BUFS) * 16 * LOADS + 16 * LOADS)
                pe.wait_ge(shift_in, slot * 16 * PARTS + 16 * PARTS)
                for kt in range(KT):
                    scores(slot, u, kt, 0)
                    if not last:
                        search(use + kt * QC, n, kt, 0)
                        search(use + kt * QC + 1, n, kt, 1)
                    if kt:
                        values(slot, u, kt - 1)
                    scores(slot, u, kt, 1)
                    if not last:
                        search(use + kt * QC + 2, n, kt, 2)
                        search(use + kt * QC + 3, n, kt, 3)
                values(slot, u, KT - 1)
                if not last:
                    turn_shift(slot + 1)
                    use = use + MAX_USES
                for c in range(FFN_USES):
                    pe.wait_ge(wide_read, use + c + 1)
                    cols = slice(c * 512, (c + 1) * 512)
                    nc.tensor.matmul(wide_ps[c % 2][:], ones3[:], bias3[:, cols], start=True, stop=False)
                    for k in range(KD):
                        mm = nc.tensor.matmul(wide_ps[c % 2][:], xt[u][:, k, :], ffnw_sb[:, k, cols], start=False, stop=(k == KD - 1))
                    mm.then_inc(wide_mm, 1)
                pe.wait_ge(o_read, slot + HEAD_BUFS + 1)
                if last:
                    pe.wait_ge(o_done, slot + 1)
                else:
                    pe.wait_ge(shift_read, slot + 2)
                for c in range(QC):
                    mm = nc.tensor.matmul(turn_ps[:, c * QC * PICK:(c + 1) * QC * PICK], o_acc[:, c * P:(c + 1) * P], pick_sb[:],
                                          start=True, stop=True)
                mm.then_inc(o_turned, 1)

            pe.wait_ge(stack_in[0], 16 * LOADS)
            for kt in range(KT):
                for j in range(QC):
                    search(kt * QC + j, 0, kt, j)
            turn_shift(0)
            with pe.Fori(0, BODIES - 1) as i:
                for u in range(HEAD_BUFS):
                    slot_work(i * HEAD_BUFS + u, i, u, False)
            for u in range(HEAD_BUFS):
                slot_work(SLOTS - HEAD_BUFS + u, BODIES - 1, u, u == HEAD_BUFS - 1)


def stage_c(nc, x, out, o_sb, ffn_sb, ident_sb, wout_sb, bout_row):
    BUFS = 4
    with ExitStack() as ctx:
        def sb(name, shape, dt=F32):
            return ctx.enter_context(nc.sbuf_tensor(name, shape, dt))

        def sem(name):
            return ctx.enter_context(nc.semaphore(name))

        x_sb = [sb(f"xc_sb{i}", [P, D]) for i in range(BUFS)]
        o_tile = [sb(f"o_tile{i}", [P, D]) for i in range(2)]
        ot_sb = [sb(f"ot_sb{i}", [P, D]) for i in range(2)]
        part_sum = [sb(f"part_sum{i}", [P, D]) for i in range(2)]
        y_sb = [sb(f"y_sb{i}", [P, D]) for i in range(BUFS)]
        ot_ps = [ctx.enter_context(nc.psum_tensor(f"ot_ps{i}", [P, D], F32)) for i in range(2)]
        y_ps = [ctx.enter_context(nc.psum_tensor(f"y_ps{i}", [P, 512], F32)) for i in range(2)]
        x_in = [sem(f"xc_in{i}") for i in range(BUFS)]
        y_out = [sem(f"y_out{i}") for i in range(BUFS)]
        tile_done = sem("tile_done")
        ot_mm = sem("ot_mm")
        ot_done = sem("ot_done")
        y_mm = sem("y_mm")
        sum_done = sem("sum_done")
        xb_done = sem("xb_done")
        y_done = sem("y_done")
        x_rows = x.rearrange("b (t p) d -> (b t) p d", p=P)
        out_rows = out.rearrange("b (t p) d -> (b t) p d", p=P)
        CC = KT // QC
        block = ctx.enter_context(nc.Block())

        @block.sync
        def _(sp):
            for c in range(BUFS):
                sp.sem_inc(y_out[c], 16)

            def load(n, c):
                sp.dma_start(x_sb[c][:], x_rows[bass.ds(n, 1)].rearrange("a p d -> (a p) d")).then_inc(x_in[c], 16)

            def store(n, c):
                sp.wait_ge(y_done, n + BUFS + 1)
                sp.dma_start(out_rows[bass.ds(n, 1)].rearrange("a p d -> (a p) d"), y_sb[c][:]).then_inc(y_out[c], 16)

            for c in range(BUFS):
                load(c, c)
            with sp.Fori(0, TILES // BUFS - 1) as i:
                for c in range(BUFS):
                    store(i * BUFS + c, c)
                    load(i * BUFS + BUFS + c, c)
            for c in range(BUFS):
                store(TILES - BUFS + c, c)
            for c in range(BUFS):
                sp.wait_ge(y_out[c], 16 * (1 + TILES // BUFS))

        @block.scalar
        def _(act):
            act.sem_inc(ot_done, 2)
            with act.Fori(0, TILES // BUFS) as i:
                for c in range(BUFS):
                    n = i * BUFS + c
                    act.wait_ge(ot_mm, n + 3)
                    act.wait_ge(y_mm, n + 1)
                    nc.scalar.copy(ot_sb[c % 2][:], ot_ps[c % 2][:]).then_inc(ot_done, 1)

        @block.gpsimd
        def _(pool):
            pool.sem_inc(xb_done, BUFS)
            with pool.Fori(0, B) as b:
                with pool.Fori(0, QC) as q:
                    for c in range(CC):
                        n = (b * QC + q) * CC + c
                        pool.wait_ge(ot_mm, n + 1)
                        nc.gpsimd.tensor_copy(o_tile[c % 2][:].rearrange("p (h a d) -> p h a d", a=1, d=DH),
                                              o_sb[:, bass.ds(b * H, H), bass.ds(q + c * QC, 1), :]).then_inc(tile_done, 1)
                        pool.wait_ge(x_in[c], (b * QC + q) * 16 + 16)
                        nc.gpsimd.tensor_tensor(x_sb[c][:], x_sb[c][:], bout_row[:], ALU.add).then_inc(xb_done, 1)

        @block.tensor
        def _(pe):
            pe.sem_inc(ot_mm, 2)
            pe.sem_inc(y_mm, 2)

            def turn(n, c):
                pe.wait_ge(tile_done, n + 1)
                pe.wait_ge(ot_done, n + 1)
                for k in range(KD):
                    last = nc.tensor.transpose(ot_ps[c % 2][:, k * P:(k + 1) * P], o_tile[c % 2][:, k * P:(k + 1) * P], ident_sb[:])
                last.then_inc(ot_mm, 1)

            def project(n, c):
                pe.wait_ge(ot_done, n + 3)
                pe.wait_ge(sum_done, n + 1)
                for k in range(KD):
                    last = nc.tensor.matmul(y_ps[c % 2][:, 0:D], ot_sb[c % 2][:, k * P:(k + 1) * P], wout_sb[:, k, :],
                                            start=(k == 0), stop=(k == KD - 1))
                last.then_inc(y_mm, 1)

            turn(0, 0)
            with pe.Fori(0, TILES // BUFS - 1) as i:
                for c in range(BUFS):
                    turn(i * BUFS + c + 1, c + 1)
                    project(i * BUFS + c, c)
            for c in range(BUFS):
                if c + 1 < BUFS:
                    turn(TILES - BUFS + c + 1, c + 1)
                project(TILES - BUFS + c, c)

        @block.vector
        def _(dve):
            dve.sem_inc(sum_done, 2)
            dve.sem_inc(y_done, BUFS)
            with dve.Fori(0, TILES // BUFS) as i:
                for c in range(BUFS):
                    n = i * BUFS + c
                    dve.wait_ge(y_mm, n + 3)
                    dve.wait_ge(y_done, n + 3)
                    nc.vector.tensor_tensor(part_sum[c % 2][:], y_ps[c % 2][:, 0:D],
                                            ffn_sb[:, bass.ds(n, 1), :].rearrange("p a d -> p (a d)"), ALU.add).then_inc(sum_done, 1)
                    dve.wait_ge(sum_done, n + 3)
                    dve.wait_ge(xb_done, n + BUFS + 1)
                    dve.wait_ge(y_out[c], i * 16 + 16)
                    nc.vector.tensor_tensor(y_sb[c][:], part_sum[c % 2][:], x_sb[c][:], ALU.add).then_inc(y_done, 1)


_INS = ["L0_attn_x", "L0_attn_w_qkv", "L0_attn_b_qkv", "L0_attn_w_out", "L0_attn_b_out", "L0_ffn_tile_sigs", "L0_ffn_W",
        "L0_ffn_b"]


def kernel(**inputs):
    import numpy as _np
    import concourse.bacc as _bacc
    from concourse import mybir as _mybir
    from concourse.bass_utils import run_bass_kernel_spmd as _run

    nc = _bacc.Bacc("TRN2", target_bir_lowering=False, num_devices=1)
    arrays, args = {}, []

    def give(name, a):
        a = _np.ascontiguousarray(a)
        arrays[name] = a
        args.append(nc.dram_tensor(name, a.shape, _mybir.dt.from_np(a.dtype), kind="ExternalInput").ap())

    for name in _INS:
        give(f"in_{name}_dram", inputs[name].T if name == "L0_ffn_tile_sigs" else inputs[name])
    give("in_bqk_cols_dram", _np.asarray(inputs["L0_attn_b_qkv"])[0:2 * D].reshape(MB, P).T)
    for name, a in zip(("rope", "ident", "swap", "pick", "rank"), build_tables()):
        give(f"table_{name}_dram", a)
    out = nc.dram_tensor("out_dram", (B, L, D), _mybir.dt.float32, kind="ExternalOutput").ap()
    routed_attention_kernel(nc, *args, out)
    r = _run(nc, [arrays], core_ids=[0])
    return r.results[0]["out_dram"]
```

```python
from contextlib import ExitStack

import numpy as np

import concourse.bass as bass
from concourse import mybir

ALU = mybir.AluOpType
ACT = mybir.ActivationFunctionType
F32 = mybir.dt.float32
BF16 = mybir.dt.bfloat16
AX_X = mybir.AxisListType.X

P = 128
B, L, D = 2, 2048, 256
H = 16
DH = D // H
T = 8
THETA = 500.0
EPS = 1e-5

TOKENS = B * L
TILES = TOKENS // P
KD = D // P
GROUP = 512
GT = GROUP // P
GROUPS = L // GROUP
MB = 2 * KD
PARTS = 3

SLOTS = B * H
KT = L // P
QC = L // 512
HEAD_BUFS = 4
WIDE = 3
LEAD = 5
P_BUFS = 3
RS = 6 * DH
PAIRS = ((0, 0), (0, 1), (0, 2), (1, 0), (1, 1), (2, 0))
RA = RS + PARTS
VW = 32


def build_tables():
    half = DH // 2
    freqs = (1.0 / np.float32(THETA) ** (np.arange(half, dtype=np.float32) / np.float32(half))).astype(np.float32)
    angles = np.arange(L, dtype=np.float32)[None, :] * freqs[:, None]
    cos, sin = np.cos(angles), np.sin(angles)
    rope = np.stack([np.concatenate([cos, cos]), np.concatenate([-sin, sin])]).astype(np.float32)
    ident = np.eye(P, dtype=np.float32)
    swap = np.zeros((P, P), np.float32)
    for m in range(P):
        head, d = divmod(m, DH)
        swap[head * DH + (d + half) % DH, m] = 1.0
    pick = np.zeros((P, QC, DH + 1), np.float32)
    for c in range(QC):
        for d in range(DH + 1):
            pick[VW * c + d, c, d] = 1.0
    rank = np.arange(T, 0, -1, dtype=np.float32)[None, :]
    return rope, ident, swap, pick.reshape(P, -1), rank


def routed_attention_kernel(nc, x, w_qkv, b_qkv, w_out, b_out, sigs_t, ffn_w, ffn_b,
                            bqk_cols, rope, ident, swap, pick, rank, out):
    parts_dram = nc.dram_tensor("qk_parts", (PARTS, 2 * D, TOKENS), BF16, kind="Internal").ap()
    xt_dram = nc.dram_tensor("xn_transposed", (TILES, P, KD, P), F32, kind="Internal").ap()
    bp_dram = nc.dram_tensor("ffn_bias_parts", (PARTS, T * D), BF16, kind="Internal").ap()

    with ExitStack() as top:
        def keep(name, shape, dt=F32):
            return top.enter_context(nc.sbuf_tensor(name, shape, dt))

        v_sb = keep("v_sb", [P, TILES, D])
        ffnw_sb = keep("ffnw_sb", [P, KD, T * D])
        onehot = keep("onehot", [P, TILES, T])
        ident_sb = keep("ident_sb", [P, P])
        pick_sb = keep("pick_sb", [P, QC * (DH + 1)])
        wout_sb = keep("wout_sb", [P, KD, D])
        bout_row = keep("bout_row", [P, D])
        bias3 = keep("bias3", [P, T * D], BF16)
        ones3 = keep("ones3", [P, P], BF16)
        ident_bf = keep("ident_bf", [P, P], BF16)

        stage_a(nc, x, w_qkv, b_qkv, w_out, b_out, sigs_t, ffn_w, ffn_b, bqk_cols, rope, ident, swap, pick, rank,
                parts_dram, xt_dram, bp_dram, v_sb, ffnw_sb, onehot, ident_sb, ident_bf, pick_sb, wout_sb,
                bout_row, bias3, ones3)
        ffn_sb = keep("ffn_sb", [P, TILES, D])
        o_sb = keep("o_sb", [P, SLOTS, KT, DH])
        stage_b(nc, parts_dram, xt_dram, v_sb, ffn_sb, o_sb, ffnw_sb, onehot, ident_bf, pick_sb, bias3, ones3)
        stage_c(nc, x, out, o_sb, ffn_sb, ident_sb, wout_sb, bout_row)


def stage_a(nc, x, w_qkv, b_qkv, w_out, b_out, sigs_t, ffn_w, ffn_b, bqk_cols, rope, ident, swap, pick, rank,
            parts_dram, xt_dram, bp_dram, v_sb, ffnw_sb, onehot, ident_sb, ident_bf, pick_sb, wout_sb,
            bout_row, bias3, ones3):
    UNITS = GROUPS * MB
    VN = D + T
    with ExitStack() as ctx:
        def sb(name, shape, dt=F32):
            return ctx.enter_context(nc.sbuf_tensor(name, shape, dt))

        def sem(name):
            return ctx.enter_context(nc.semaphore(name))

        wqk_sb = sb("wqk_sb", [P, KD, 2 * D])
        wvs_sb = sb("wvs_sb", [P, KD, VN])
        sig_sb = sb("sig_sb", [P, KD, T])
        sneg = sb("sneg", [P, KD, T])
        spos = sb("spos", [P, KD, T])
        swap_sb = sb("swap_sb", [P, P])
        cos_sb = sb("cos_sb", [P, L])
        sin_sb = sb("sin_sb", [P, L])
        bqk_raw = sb("bqk_raw", [P, MB])
        bqk = sb("bqk", [P, MB])
        bv_row = sb("bv_row", [P, D])
        rank_row = sb("rank_row", [P, T])
        eps_col = sb("eps_col", [P, 1])
        x_sb = [sb(f"x_sb{i}", [P, GT, D]) for i in range(2)]
        xn_sb = [sb(f"xn_sb{i}", [P, GT, D]) for i in range(2)]
        xt_sb = [sb(f"xt_sb{i}", [P, KD, GROUP]) for i in range(2)]
        stats = sb("stats", [P, GT, 6])
        count_seen = sb("count_seen", [P, 1])
        moments = sb("moments", [P, GT, 2])
        std = sb("std", [P, GT])
        rstd = sb("rstd", [P, GT])
        gate = sb("gate", [P, GT, T])
        gmax = sb("gmax", [P, GT])
        ranked = sb("ranked", [P, GT, T])
        first = sb("first", [P, GT])
        qk_sb = [sb(f"qk_sb{i}", [P, GROUP]) for i in range(2)]
        qcos = [sb(f"qcos{i}", [P, GROUP]) for i in range(2)]
        qsin = [sb(f"qsin{i}", [P, GROUP]) for i in range(2)]
        roped = [sb(f"roped{i}", [P, GROUP]) for i in range(2)]
        rest = [sb(f"rest{i}", [P, GROUP]) for i in range(4)]
        fb_sb = sb("fb_sb", [P, T * D // P])
        fb_rest = sb("fb_rest", [P, 2, T * D // P])
        fb_parts = sb("fb_parts", [P, PARTS, T * D // P], BF16)
        parts = [sb(f"parts{i}", [P, PARTS, MB, GROUP], BF16) for i in range(2)]

        xt_ps = [ctx.enter_context(nc.psum_tensor(f"xt_ps{k}", [P, GROUP], F32)) for k in range(KD)]
        qk_ps = [ctx.enter_context(nc.psum_tensor(f"qk_ps{k}", [P, GROUP], F32)) for k in range(2)]
        sw_ps = [ctx.enter_context(nc.psum_tensor(f"sw_ps{k}", [P, GROUP], F32)) for k in range(2)]
        v_ps = [ctx.enter_context(nc.psum_tensor(f"v_ps{k}", [P, 512], F32)) for k in range(2)]

        weights_in = sem("weights_in")
        late_in = sem("late_in")
        x_in = [sem(f"x_in{i}") for i in range(2)]
        consts_done = sem("consts_done")
        signs_done = sem("signs_done")
        bparts_done = sem("bparts_done")
        bparts_out = sem("bparts_out")
        stats_done = sem("stats_done")
        moments_done = sem("moments_done")
        std_done = sem("std_done")
        rstd_done = sem("rstd_done")
        xn_done = sem("xn_done")
        xt_mm = sem("xt_mm")
        xt_done = sem("xt_done")
        xt_out = [sem(f"xt_out{i}") for i in range(2)]
        qk_mm = sem("qk_mm")
        qk_done = sem("qk_done")
        v_mm = sem("v_mm")
        v_done = sem("v_done")
        gate_step = sem("gate_step")
        swap_mm = sem("swap_mm")
        qcos_done = sem("qcos_done")
        qsin_done = sem("qsin_done")
        roped_done = sem("roped_done")
        hi_done = sem("hi_done")
        rest_done = sem("rest_done")
        mid_done = sem("mid_done")
        lo_done = sem("lo_done")
        parts_out = [sem(f"parts_out{i}") for i in range(2)]

        x_view = x.rearrange("b (g t p) d -> b g p t d", t=GT, p=P)
        xt_view = xt_dram.rearrange("(n t) p k q -> n p k t q", t=GT)
        gp_consts = sem("gp_consts")
        N_WEIGHTS = 9 + 2 * (P // DH)
        block = ctx.enter_context(nc.Block())


        @block.sync
        def _(sp):
            def load_x(b, g):
                sp.wait_ge(xn_done, b * GROUPS + g + 1)
                sp.dma_start(x_sb[g % 2][:], x_view[bass.ds(b, 1), g].rearrange("a p t d -> (a p) t d")).then_inc(x_in[g % 2], 16)

            def const(to, of, signal):
                sp.dma_start(to, of).then_inc(signal, 16)

            for i in range(2):
                sp.sem_inc(xt_out[i], 16)
                sp.sem_inc(parts_out[i], 16)
            const(ident_sb[:], ident, weights_in)
            const(wqk_sb[:], w_qkv[:, 0:2 * D].rearrange("(k p) n -> p k n", p=P), weights_in)
            const(bqk_raw[:], bqk_cols, weights_in)
            const(wvs_sb[:, :, 0:D], w_qkv[:, 2 * D:3 * D].rearrange("(k p) n -> p k n", p=P), weights_in)
            const(sig_sb[:], sigs_t.rearrange("(k p) t -> p k t", p=P), weights_in)
            const(swap_sb[:], swap, weights_in)
            const(bv_row[:], b_qkv[2 * D:3 * D].partition_broadcast(P), weights_in)
            const(rank_row[:], rank[0, :].partition_broadcast(P), weights_in)
            const(fb_sb[:], ffn_b.rearrange("t d -> (t d)").rearrange("(p n) -> p n", p=P), weights_in)
            for n, table in enumerate((cos_sb, sin_sb)):
                for h in range(P // DH):
                    const(table[h * DH:(h + 1) * DH, :], rope[n], weights_in)
            with sp.Fori(0, B) as b:
                load_x(b, 0)
                load_x(b, 1)
                for g in range(GROUPS):
                    G = b * GROUPS + g
                    if g + 2 < GROUPS:
                        load_x(b, g + 2)
                    sp.wait_ge(xt_done, G + 2)
                    for k in range(KD):
                        sp.dma_start(xt_view[bass.ds(G, 1), :, k].rearrange("n p t q -> (n p) t q"),
                                     xt_sb[g % 2][:, k, :].rearrange("p (t q) -> p t q", q=P)).then_inc(xt_out[g % 2], 16)
                    sp.wait_ge(lo_done, (G + 1) * MB + 4)
                    for a in range(PARTS):
                        sp.dma_start(parts_dram[a].rearrange("(m p) n -> p m n", p=P)[:, :, bass.ds(G * GROUP, GROUP)],
                                     parts[g % 2][:, a]).then_inc(parts_out[g % 2], 16)
            for k in range(KD):
                const(ffnw_sb[:, k].rearrange("p (t n) -> p t n", t=T), ffn_w[:, k * P:(k + 1) * P, :].rearrange("t p n -> p t n"), late_in)
            const(wout_sb[:], w_out.rearrange("(k p) n -> p k n", p=P), late_in)
            const(pick_sb[:], pick, late_in)
            const(bout_row[:], b_out.partition_broadcast(P), late_in)
            sp.wait_ge(bparts_done, 5)
            for a in range(PARTS):
                sp.dma_start(bp_dram[a].rearrange("(p n) -> p n", p=P), fb_parts[:, a]).then_inc(bparts_out, 16)
            sp.wait_ge(bparts_out, 16 * PARTS)
            const(bias3[0:PARTS, :], bp_dram, late_in)
            sp.wait_ge(late_in, 16 * (KD + 4))
            for i in range(2):
                sp.wait_ge(xt_out[i], 16 * (1 + KD * B * GROUPS // 2))
                sp.wait_ge(parts_out[i], 16 * (1 + PARTS * B * GROUPS // 2))

        @block.scalar
        def _(act):
            act.sem_inc(xt_done, 1)
            act.sem_inc(qk_done, 2)
            act.wait_ge(consts_done, 3)
            with act.Fori(0, B) as b:
                def std_dev(g):
                    act.wait_ge(moments_done, b * GROUPS + g + 1)
                    nc.scalar.activation(std[:], moments[:, :, 1], ACT.Sqrt, bias=eps_col[:]).then_inc(std_done, 1)

                def copy_xt(g):
                    G = b * GROUPS + g
                    act.wait_ge(xt_mm, G + 3)
                    act.wait_ge(v_mm, G * GT + 4)
                    act.wait_ge(xt_out[g % 2], (b * (GROUPS // 2) + g // 2) * 16 * KD + 16)
                    for k in range(KD):
                        last = nc.scalar.copy(xt_sb[g % 2][:, k, :], xt_ps[k][:])
                    last.then_inc(xt_done, 1)

                def add_bias(s):
                    n, m = b * UNITS + s, s % MB
                    act.wait_ge(qk_mm, n + 1)
                    act.wait_ge(swap_mm, n + 1)
                    act.wait_ge(qcos_done, n + 1)
                    nc.scalar.activation(qk_sb[s % 2][:], qk_ps[s % 2][:], ACT.Identity, bias=bqk[:, m:m + 1],
                                         scale=1.0 if m < KD else float(DH) ** -0.5).then_inc(qk_done, 1)

                def hi_part(s):
                    g, m = divmod(s, MB)
                    act.wait_ge(roped_done, b * UNITS + s + 3)
                    if m == 0:
                        act.wait_ge(parts_out[g % 2], (b * (GROUPS // 2) + g // 2) * 16 * PARTS + 16)
                    nc.scalar.copy(parts[g % 2][:, 0, m, :], roped[s % 2][:]).then_inc(hi_done, 1)

                def mid_part(s):
                    g, m = divmod(s, MB)
                    act.wait_ge(rest_done, b * UNITS + s + 3)
                    nc.scalar.copy(parts[g % 2][:, 1, m, :], rest[s % 4][:]).then_inc(mid_done, 1)

                std_dev(0)
                copy_xt(0)
                for s in range(UNITS + 3):
                    g, m = divmod(s, MB)
                    if m == 1 and g + 1 < GROUPS:
                        std_dev(g + 1)
                    if s < UNITS:
                        add_bias(s)
                    if 2 <= s < UNITS + 2:
                        hi_part(s - 2)
                    if 3 <= s:
                        mid_part(s - 3)
                    if m == 3 and g + 1 < GROUPS:
                        copy_xt(g + 1)

        @block.gpsimd
        def _(pool):
            pool.sem_inc(qcos_done, 2)
            pool.sem_inc(rest_done, 2)
            pool.memset(bias3[:], 0.0).then_inc(gp_consts, 1)
            pool.memset(ones3[:], 1.0).then_inc(gp_consts, 1)
            pool.wait_ge(weights_in, 16 * N_WEIGHTS)
            with pool.Fori(0, B) as b:
                for s in range(UNITS + 2):
                    if s < UNITS:
                        n, g = b * UNITS + s, s // MB
                        pool.wait_ge(qk_done, n + 3)
                        pool.wait_ge(roped_done, n + 1)
                        nc.gpsimd.tensor_tensor(qcos[s % 2][:], qk_sb[s % 2][:], cos_sb[:, g * GROUP:(g + 1) * GROUP],
                                                ALU.mult).then_inc(qcos_done, 1)
                    if s >= 2:
                        n, g, m = b * UNITS + s - 2, (s - 2) // MB, (s - 2) % MB
                        pool.wait_ge(hi_done, n + 1)
                        pool.wait_ge(lo_done, n + 1)
                        nc.gpsimd.tensor_tensor(rest[(s - 2) % 4][:], roped[s % 2][:], parts[g % 2][:, 0, m, :],
                                                ALU.subtract).then_inc(rest_done, 1)

        @block.vector
        def _(dve):
            dve.sem_inc(xn_done, 2)
            dve.sem_inc(roped_done, 2)
            dve.sem_inc(qsin_done, 2)
            dve.sem_inc(lo_done, 4)
            dve.sem_inc(v_done, 2)
            dve.memset(eps_col[:], EPS).then_inc(consts_done, 1)
            dve.wait_ge(weights_in, 16 * N_WEIGHTS)
            nc.vector.tensor_scalar(spos[:], sig_sb[:], 0.0, None, ALU.is_gt).then_inc(signs_done, 1)
            nc.vector.tensor_scalar(sneg[:], sig_sb[:], 0.0, None, ALU.is_lt).then_inc(signs_done, 1)
            dve.wait_ge(signs_done, 2)
            nc.vector.tensor_tensor(wvs_sb[:, :, D:VN], spos[:], sneg[:], ALU.subtract).then_inc(signs_done, 1)
            nc.vector.tensor_copy(bqk[:, 0:KD], bqk_raw[:, 0:KD]).then_inc(consts_done, 1)
            nc.vector.tensor_scalar(bqk[:, KD:MB], bqk_raw[:, KD:MB], float(DH) ** -0.5, None, ALU.mult).then_inc(consts_done, 1)
            nc.vector.tensor_copy(ident_bf[:], ident_sb[:]).then_inc(consts_done, 1)
            nc.vector.tensor_copy(fb_parts[:, 0], fb_sb[:]).then_inc(bparts_done, 1)
            dve.wait_ge(bparts_done, 1)
            nc.vector.tensor_tensor(fb_rest[:, 0], fb_sb[:], fb_parts[:, 0], ALU.subtract).then_inc(bparts_done, 1)
            dve.wait_ge(bparts_done, 2)
            nc.vector.tensor_copy(fb_parts[:, 1], fb_rest[:, 0]).then_inc(bparts_done, 1)
            dve.wait_ge(bparts_done, 3)
            nc.vector.tensor_tensor(fb_rest[:, 1], fb_rest[:, 0], fb_parts[:, 1], ALU.subtract).then_inc(bparts_done, 1)
            dve.wait_ge(bparts_done, 4)
            nc.vector.tensor_copy(fb_parts[:, 2], fb_rest[:, 1]).then_inc(bparts_done, 1)

            with dve.Fori(0, B) as b:
                def norm(g):
                    G = b * GROUPS + g
                    dve.wait_ge(x_in[g % 2], (b * (GROUPS // 2) + g // 2) * 16 + 16)
                    for t in range(GT):
                        last = nc.vector.bn_stats(stats[:, t, :], x_sb[g % 2][:, t, :])
                    last.then_inc(stats_done, 1)
                    dve.wait_ge(stats_done, G + 1)
                    nc.vector.tensor_copy(count_seen[:], stats[:, 0, 0:1])
                    for t in range(GT):
                        last = nc.vector.bn_aggr(moments[:, t, :], stats[:, t, :])
                    last.then_inc(moments_done, 1)
                    dve.wait_ge(std_done, G + 1)
                    nc.vector.reciprocal(rstd[:], std[:]).then_inc(rstd_done, 1)
                    dve.wait_ge(rstd_done, G + 1)
                    dve.wait_ge(xt_mm, G + 1)
                    for t in range(GT):
                        last = nc.vector.tensor_scalar(xn_sb[g % 2][:, t, :], x_sb[g % 2][:, t, :], moments[:, t, 0:1],
                                                       rstd[:, t:t + 1], ALU.subtract, ALU.mult)
                    last.then_inc(xn_done, 1)

                def take_v(s):
                    n, t = b * GROUPS * GT + s, s % GT
                    dve.wait_ge(v_mm, n + 1 + 8)
                    nc.vector.tensor_tensor(v_sb[:, bass.ds(n, 1), :].rearrange("p a d -> p (a d)"), v_ps[s % 2][:, 0:D],
                                            bv_row[:], ALU.add)
                    nc.vector.tensor_copy(gate[:, t, :], v_ps[s % 2][:, D:VN]).then_inc(v_done, 1)

                def route(g):
                    G = b * GROUPS + g
                    dve.wait_ge(v_done, (G + 1) * GT + 2)
                    nc.vector.tensor_reduce(gmax[:], gate[:], AX_X, ALU.max).then_inc(gate_step, 1)
                    dve.wait_ge(gate_step, G * 4 + 1)
                    for t in range(GT):
                        last = nc.vector.scalar_tensor_tensor(ranked[:, t, :], gate[:, t, :], gmax[:, t:t + 1], rank_row[:],
                                                              ALU.is_equal, ALU.mult)
                    last.then_inc(gate_step, 1)
                    dve.wait_ge(gate_step, G * 4 + 2)
                    nc.vector.tensor_reduce(first[:], ranked[:], AX_X, ALU.max).then_inc(gate_step, 1)
                    dve.wait_ge(gate_step, G * 4 + 3)
                    for t in range(GT):
                        last = nc.vector.tensor_scalar(onehot[:, bass.ds(G * GT + t, 1), :].rearrange("p a e -> p (a e)"),
                                                       rank_row[:], first[:, t:t + 1], None, ALU.is_equal)
                    last.then_inc(gate_step, 1)

                def rope_sum(s):
                    n, g = b * UNITS + s, s // MB
                    dve.wait_ge(swap_mm, n + 3)
                    dve.wait_ge(roped_done, n + 1)
                    nc.vector.tensor_tensor(qsin[s % 2][:], sw_ps[s % 2][:], sin_sb[:, g * GROUP:(g + 1) * GROUP],
                                            ALU.mult).then_inc(qsin_done, 1)
                    dve.wait_ge(qcos_done, n + 3)
                    dve.wait_ge(qsin_done, n + 3)
                    dve.wait_ge(rest_done, n + 1)
                    nc.vector.tensor_tensor(roped[s % 2][:], qcos[s % 2][:], qsin[s % 2][:], ALU.add).then_inc(roped_done, 1)

                def lo_part(s):
                    n, g, m = b * UNITS + s, s // MB, s % MB
                    dve.wait_ge(rest_done, n + 3)
                    dve.wait_ge(mid_done, n + 1)
                    nc.vector.tensor_tensor(parts[g % 2][:, 2, m, :], rest[s % 4][:], parts[g % 2][:, 1, m, :],
                                            ALU.subtract).then_inc(lo_done, 1)

                norm(0)
                for s in range(1, UNITS + 4):
                    if s % MB == 1 and s > MB:
                        route(s // MB - 1)
                    if s <= UNITS:
                        take_v(s - 1)
                        rope_sum(s - 1)
                    if 4 <= s < UNITS + 4:
                        lo_part(s - 4)
                    if s % MB == 1 and s // MB + 1 < GROUPS:
                        norm(s // MB + 1)

        @block.tensor
        def _(pe):
            pe.sem_inc(xt_mm, 2)
            pe.sem_inc(swap_mm, 2)
            pe.sem_inc(v_mm, 8)
            pe.wait_ge(weights_in, 16 * N_WEIGHTS)
            pe.wait_ge(signs_done, 3)
            with pe.Fori(0, B) as b:
                def transposes(g):
                    G = b * GROUPS + g
                    pe.wait_ge(xn_done, G + 3)
                    pe.wait_ge(xt_done, G + 1)
                    for k in range(KD):
                        for t in range(GT):
                            last = nc.tensor.transpose(xt_ps[k][:, t * P:(t + 1) * P], xn_sb[g % 2][:, t, k * P:(k + 1) * P],
                                                       ident_sb[:])
                    last.then_inc(xt_mm, 1)

                def project(s):
                    g, m = divmod(s, MB)
                    if m == 0:
                        pe.wait_ge(xt_done, b * GROUPS + g + 2)
                    pe.wait_ge(qk_done, b * UNITS + s + 1)
                    for k in range(KD):
                        last = nc.tensor.matmul(qk_ps[s % 2][:], wqk_sb[:, k, m * P:(m + 1) * P], xt_sb[g % 2][:, k, :],
                                                start=(k == 0), stop=(k == KD - 1))
                    last.then_inc(qk_mm, 1)

                def project_v(s):
                    g, t = divmod(s, GT)
                    pe.wait_ge(v_done, b * GROUPS * GT + s + 1)
                    for k in range(KD):
                        last = nc.tensor.matmul(v_ps[s % 2][:, 0:VN], xt_sb[g % 2][:, k, t * P:(t + 1) * P], wvs_sb[:, k, :],
                                                start=(k == 0), stop=(k == KD - 1))
                    last.then_inc(v_mm, 1)

                def swap_halves(s):
                    pe.wait_ge(qk_done, b * UNITS + s + 3)
                    pe.wait_ge(qsin_done, b * UNITS + s + 1)
                    nc.tensor.matmul(sw_ps[s % 2][:], swap_sb[:], qk_sb[s % 2][:], start=True, stop=True).then_inc(swap_mm, 1)

                transposes(0)
                for s in range(UNITS + 1):
                    if s < UNITS:
                        project(s)
                    if s >= 1:
                        project_v(s - 1)
                        swap_halves(s - 1)
                    if s % MB == MB - 1 and s // MB + 1 < GROUPS:
                        transposes(s // MB + 1)


def stage_b(nc, parts_dram, xt_dram, v_sb, ffn_sb, o_sb, ffnw_sb, onehot, ident_bf, pick_sb, bias3, ones3):
    PICK = DH + 1
    SHIFT = PARTS * KT
    LOADS = 2 * len(PAIRS) + 1
    FFN_USES = T * D // 512
    FFN_AT = {3: 0, 5: 1, 7: 2, 9: 3}
    O_AT = 2
    TURN_AT = KT - LEAD + 1
    USES = KT * QC + FFN_USES + 2
    FIRST_USES = (KT + LEAD) * QC + 1
    BODIES = SLOTS // HEAD_BUFS
    with ExitStack() as ctx:
        def sb(name, shape, dt=F32):
            return ctx.enter_context(nc.sbuf_tensor(name, shape, dt))

        def psum(name, shape):
            return ctx.enter_context(nc.psum_tensor(name, shape, F32))

        def sem(name):
            return ctx.enter_context(nc.semaphore(name))

        q_st = [sb(f"q_st{i}", [P, L], BF16) for i in range(HEAD_BUFS)]
        k_st = [sb(f"k_st{i}", [P, L], BF16) for i in range(HEAD_BUFS)]
        vh = [sb(f"vh{i}", [P, KT, VW]) for i in range(HEAD_BUFS)]
        xt = [sb(f"xt{i}", [P, KD, P]) for i in range(HEAD_BUFS)]
        probs = [sb(f"probs{i}", [P, L]) for i in range(P_BUFS)]
        chunk_max = [sb(f"chunk_max{i}", [P, KT, QC]) for i in range(2)]
        neg_max = sb("neg_max", [P, KT])
        shift = sb("shift", [P, P], BF16)
        shift_rest = sb("shift_rest", [P, 2, KT])
        shift_rows = sb("shift_rows", [SHIFT, P], BF16)
        o_acc = sb("o_acc", [P, 512])
        rden = sb("rden", [P, KT])

        st_ps = [psum(f"st_ps{i}", [P, L // 2]) for i in range(2)]
        wide_ps = [psum(f"wide_ps{i}", [P, 512]) for i in range(WIDE)]
        o_ps = psum("o_ps", [P, 512])

        stack_in = [sem(f"stack_in{i}") for i in range(HEAD_BUFS)]
        ones_done = sem("ones_done")
        rows_set = sem("rows_set")
        vh_done = sem("vh_done")
        shift_in = sem("shift_in")
        st_mm = sem("st_mm")
        exp_done = sem("exp_done")
        pv_mm = sem("pv_mm")
        o_read = sem("o_read")
        o_turned = sem("o_turned")
        o_done = sem("o_done")
        wide_mm = sem("wide_mm")
        wide_read = sem("wide_read")
        shift_step = sem("shift_step")
        shift_read = sem("shift_read")
        ffn_step = sem("ffn_step")
        rden_done = sem("rden_done")
        block = ctx.enter_context(nc.Block())

        def target(kt):
            return 1 + (kt + LEAD) // KT, (kt + LEAD) % KT

        def bodies(engine, slot_work):
            for u in range(HEAD_BUFS):
                slot_work(u, 0, u)
            with engine.Fori(1, BODIES - 1) as i:
                for u in range(HEAD_BUFS):
                    slot_work(i * HEAD_BUFS + u, i, u)
            for u in range(HEAD_BUFS):
                slot_work(SLOTS - HEAD_BUFS + u, BODIES - 1, u)

        def known(slot, n):
            return isinstance(slot, int) and slot == n

        def searched(slot, kt):
            return not (isinstance(slot, int) and slot + target(kt)[0] >= SLOTS)

        def uses_in(slot):
            return (USES - (slot == 0) - (slot == SLOTS - 1)
                    - QC * sum(not searched(slot, kt) for kt in range(KT)))

        def base(slot):
            if isinstance(slot, int):
                return FIRST_USES + sum(uses_in(n) for n in range(slot))
            return slot * USES + (FIRST_USES - 1)

        def free_at(slot, k):
            if k >= WIDE:
                return base(slot) + k - WIDE + 1
            if isinstance(slot, int):
                return base(slot)
            return base(slot) + max(m for m in range(USES) if m % WIDE == k) - USES + 1

        @block.sync
        def _(sp):
            def load_slot(b, h, slot, u):
                if not known(slot, u):
                    sp.wait_ge(o_read, slot - HEAD_BUFS + 1)
                row, cols = h * DH, slice(b * L, (b + 1) * L)
                for r, (qa, ka) in enumerate(PAIRS):
                    sp.dma_start(q_st[u][r * DH:(r + 1) * DH, :], parts_dram[qa, bass.ds(row, DH), cols]).then_inc(stack_in[u], 16)
                    sp.dma_start(k_st[u][r * DH:(r + 1) * DH, :], parts_dram[ka, bass.ds(row + D, DH), cols]).then_inc(stack_in[u], 16)
                sp.dma_start(xt[u][:], xt_dram[bass.ds(slot, 1)].rearrange("n p k q -> (n p) k q")).then_inc(stack_in[u], 16)

            for u in range(HEAD_BUFS):
                load_slot(0, u, u, u)
            for b in range(B):
                with sp.Fori(1 - b, H // HEAD_BUFS) as j:
                    for u in range(HEAD_BUFS):
                        load_slot(b, j * HEAD_BUFS + u, j * HEAD_BUFS + (b * H + u), u)

        @block.gpsimd
        def _(pool):
            for i in range(HEAD_BUFS):
                pool.memset(vh[i][:], 0.0).then_inc(ones_done, 1)
            pool.wait_ge(ones_done, HEAD_BUFS)
            for i in range(HEAD_BUFS):
                pool.memset(vh[i][:, :, DH:DH + 1], 1.0).then_inc(ones_done, 1)
            pool.wait_ge(ones_done, 2 * HEAD_BUFS)

            def take_v(b, h, slot, u):
                if not known(slot, u):
                    pool.wait_ge(o_read, slot - HEAD_BUFS + 1)
                nc.gpsimd.tensor_copy(vh[u][:, :, 0:DH], v_sb[:, b * KT:(b + 1) * KT, bass.ds(h * DH, DH)]).then_inc(vh_done, 1)

            for u in range(HEAD_BUFS):
                take_v(0, u, u, u)
            for b in range(B):
                with pool.Fori(1 - b, H // HEAD_BUFS) as j:
                    for u in range(HEAD_BUFS):
                        take_v(b, j * HEAD_BUFS + u, j * HEAD_BUFS + (b * H + u), u)

        @block.scalar
        def _(act):
            def load_shift(slot, u):
                act.wait_ge(shift_read, slot + 1)
                for a in range(PARTS):
                    act.dma_start(q_st[u][RS + a:RS + a + 1, :].rearrange("a (t q) -> a t q", q=P),
                                  shift_rows[a * KT:(a + 1) * KT, :]).then_inc(shift_in, 16)

            def slot_work(slot, i, u):
                for kt in range(KT):
                    if kt >= P_BUFS:
                        act.wait_ge(pv_mm, slot * KT + kt - P_BUFS + 1)
                    for half in range(2):
                        act.wait_ge(st_mm, slot * 2 * KT + 2 * kt + half + 1)
                        nc.scalar.activation(probs[kt % P_BUFS][:, half * (L // 2):(half + 1) * (L // 2)], st_ps[half][:],
                                             ACT.Exp).then_inc(exp_done, 1)
                    if kt == TURN_AT + 1 and not known(slot, SLOTS - 1):
                        load_shift(slot + 1, (u + 1) % HEAD_BUFS)
                act.wait_ge(pv_mm, slot * KT + KT)
                nc.scalar.copy(o_acc[:], o_ps[:]).then_inc(o_read, 1)

            load_shift(0, 0)
            bodies(act, slot_work)

        @block.vector
        def _(dve):
            dve.memset(shift[:], 0.0).then_inc(rows_set, 1)
            for i in range(HEAD_BUFS):
                dve.memset(k_st[i][RS:RA, :], 1.0).then_inc(rows_set, 1)
            dve.wait_ge(rows_set, 1 + HEAD_BUFS)

            def take_max(slot_base, k, maxima, qt, j):
                dve.wait_ge(wide_mm, slot_base + k + 1)
                nc.vector.tensor_reduce(maxima[:, qt, j:j + 1], wide_ps[k % WIDE][:], AX_X, ALU.max).then_inc(wide_read, 1)

            def shift_chain(step, slot, maxima, last_read):
                part = [shift[:, a * KT:(a + 1) * KT] for a in range(PARTS)]
                if step == 0:
                    dve.wait_ge(wide_read, last_read)
                    ins = nc.vector.tensor_reduce(neg_max[:], maxima[:], AX_X, ALU.max, negate=True)
                else:
                    dve.wait_ge(shift_step, slot * 6 + step)
                    if step == 1:
                        ins = nc.vector.tensor_copy(part[0], neg_max[:])
                    elif step == 2:
                        ins = nc.vector.tensor_tensor(shift_rest[:, 0, :], neg_max[:], part[0], ALU.subtract)
                    elif step == 3:
                        ins = nc.vector.tensor_copy(part[1], shift_rest[:, 0, :])
                    elif step == 4:
                        ins = nc.vector.tensor_tensor(shift_rest[:, 1, :], shift_rest[:, 0, :], part[1], ALU.subtract)
                    else:
                        ins = nc.vector.tensor_copy(part[2], shift_rest[:, 1, :])
                ins.then_inc(shift_step, 1)

            def take_shift(slot, use, k):
                if not known(slot, 0):
                    dve.wait_ge(shift_in, slot * 16 * PARTS)
                dve.wait_ge(wide_mm, use)
                nc.vector.tensor_copy(shift_rows[:], wide_ps[k % WIDE][:].bitcast(BF16)[0:SHIFT, 0:P]).then_inc(shift_read, 1)
                dve.wait_ge(shift_read, slot + 1)
                dve.sem_inc(wide_read, 1)

            def take_o(slot, use, k):
                turned = wide_ps[k % WIDE][:, 0:KT * PICK].rearrange("p (t d) -> p t d", d=PICK)
                dve.wait_ge(wide_mm, use)
                nc.vector.reciprocal(rden[:], turned[:, :, DH]).then_inc(rden_done, 1)
                dve.wait_ge(rden_done, slot + 1)
                nc.vector.tensor_tensor(o_sb[:, bass.ds(slot, 1)].rearrange("p a t d -> p (a t) d"), turned[:, :, 0:DH],
                                        rden[:].unsqueeze(2).broadcast_to([P, KT, DH]), ALU.mult).then_inc(wide_read, 1)

            def take_ffn(slot, use, k, c):
                out = ffn_sb[:, bass.ds(slot, 1), :].rearrange("p a d -> p (a d)")
                for half in range(2):
                    e = 2 * c + half
                    mask = onehot[:, bass.ds(slot, 1), e:e + 1].rearrange("p a e -> p (a e)")
                    of = wide_ps[k % WIDE][:, half * D:(half + 1) * D]
                    if half == 0:
                        dve.wait_ge(wide_mm, use)
                        if c > 0:
                            dve.wait_ge(wide_read, use - 1)
                    else:
                        dve.wait_ge(ffn_step, slot * FFN_USES + c + 1)
                    if e == 0:
                        ins = nc.vector.tensor_scalar(out, of, mask, None, ALU.mult)
                    else:
                        ins = nc.vector.scalar_tensor_tensor(out, of, mask, out, ALU.mult, ALU.add)
                    ins.then_inc(wide_read if half else ffn_step, 1)

            def slot_work(slot, i, u):
                first, k, maxima = base(slot), 0, chunk_max[(u + 1) % 2]
                last_read = None
                for kt in range(KT):
                    ahead, qt = target(kt)
                    for j in range(QC):
                        if searched(slot, kt):
                            take_max(first, k, chunk_max[(u + ahead) % 2], qt, j)
                            k += 1
                        step = (kt - (KT - LEAD)) * QC + j
                        if 0 <= step < 6 and not known(slot, SLOTS - 1):
                            shift_chain(step, slot + 1, maxima, last_read)
                    if kt == KT - LEAD - 1:
                        last_read = first + k
                    if kt == O_AT and not known(slot, 0):
                        take_o(slot - 1, first + k + 1, k)
                        k += 1
                    if kt in FFN_AT:
                        take_ffn(slot, first + k + 1, k, FFN_AT[kt])
                        k += 1
                    if kt == TURN_AT and not known(slot, SLOTS - 1):
                        take_shift(slot + 1, first + k + 1, k)
                        k += 1

            k = 0
            for qt in range(KT + LEAD):
                for j in range(QC):
                    take_max(0, k, chunk_max[qt // KT], qt % KT, j)
                    k += 1
                if qt == KT - 1:
                    for step in range(6):
                        shift_chain(step, 0, chunk_max[0], k)
                if qt == KT:
                    take_shift(0, k + 1, k)
                    k += 1
            bodies(dve, slot_work)
            take_o(SLOTS - 1, base(SLOTS) + 1, 0)

        @block.tensor
        def _(pe):
            pe.wait_ge(ones_done, 2 * HEAD_BUFS)
            pe.wait_ge(rows_set, 1 + HEAD_BUFS)

            def search(k, n, qt, j):
                nc.tensor.matmul(wide_ps[k % WIDE][:], q_st[n][0:RS, qt * P:(qt + 1) * P], k_st[n][0:RS, j * 512:(j + 1) * 512],
                                 start=True, stop=True).then_inc(wide_mm, 1)

            def scores(slot, u, kt, half):
                if not (known(slot, 0) and kt == 0):
                    pe.wait_ge(exp_done, slot * 2 * KT + 2 * kt + half - 1)
                for c in range(2):
                    q0 = half * (L // 2) + c * 512
                    last = nc.tensor.matmul(st_ps[half][:, c * 512:(c + 1) * 512], k_st[u][0:RA, kt * P:(kt + 1) * P],
                                            q_st[u][0:RA, q0:q0 + 512], start=True, stop=True)
                last.then_inc(st_mm, 1)

            def values(slot, u, kt):
                if kt == 0:
                    if not known(slot, 0):
                        pe.wait_ge(o_read, slot)
                    pe.wait_ge(vh_done, slot + 1)
                pe.wait_ge(exp_done, slot * 2 * KT + 2 * kt + 2)
                for c in range(QC):
                    last = nc.tensor.matmul(o_ps[VW * c:VW * (c + 1), :], vh[u][:, kt, :], probs[kt % P_BUFS][:, c * 512:(c + 1) * 512],
                                            start=(kt == 0), stop=(kt == KT - 1), tile_position=(0, VW * c))
                last.then_inc(pv_mm, 1)

            def turn_shift(slot, k):
                pe.wait_ge(shift_step, slot * 6 + 6)
                nc.tensor.transpose(wide_ps[k % WIDE][:].bitcast(BF16)[:, 0:P], shift[:], ident_bf[:]).then_inc(wide_mm, 1)

            def turn_o(slot, k):
                pe.wait_ge(o_read, slot + 1)
                for c in range(QC):
                    mm = nc.tensor.matmul(wide_ps[k % WIDE][:, c * QC * PICK:(c + 1) * QC * PICK], o_acc[:, c * P:(c + 1) * P],
                                          pick_sb[:], start=True, stop=True)
                mm.then_inc(wide_mm, 1)

            def feed_forward(k, u, c):
                cols = slice(c * 512, (c + 1) * 512)
                nc.tensor.matmul(wide_ps[k % WIDE][:], ones3[:], bias3[:, cols], start=True, stop=False)
                for a in range(KD):
                    mm = nc.tensor.matmul(wide_ps[k % WIDE][:], xt[u][:, a, :], ffnw_sb[:, a, cols], start=False, stop=(a == KD - 1))
                mm.then_inc(wide_mm, 1)

            def slot_work(slot, i, u):
                k = 0
                pe.wait_ge(shift_in, (slot + 1) * 16 * PARTS)
                for kt in range(KT):
                    ahead, qt = target(kt)
                    n = (u + ahead) % HEAD_BUFS
                    if qt == 0 and searched(slot, kt):
                        pe.wait_ge(stack_in[n], (i + (u + ahead) // HEAD_BUFS + 1) * 16 * LOADS)
                    for j in range(QC):
                        if searched(slot, kt):
                            pe.wait_ge(wide_read, free_at(slot, k))
                            search(k, n, qt, j)
                            k += 1
                        if j < 2:
                            scores(slot, u, kt, j)
                        if j == 2 and kt:
                            values(slot, u, kt - 1)
                    if kt == O_AT and not known(slot, 0):
                        pe.wait_ge(wide_read, free_at(slot, k))
                        turn_o(slot - 1, k)
                        k += 1
                    if kt in FFN_AT:
                        pe.wait_ge(wide_read, free_at(slot, k))
                        feed_forward(k, u, FFN_AT[kt])
                        k += 1
                    if kt == TURN_AT and not known(slot, SLOTS - 1):
                        pe.wait_ge(wide_read, free_at(slot, k))
                        turn_shift(slot + 1, k)
                        k += 1
                values(slot, u, KT - 1)

            k = 0
            for qt in range(KT + LEAD):
                if qt % KT == 0:
                    pe.wait_ge(stack_in[qt // KT], 16 * LOADS)
                for j in range(QC):
                    if k >= WIDE:
                        pe.wait_ge(wide_read, k - WIDE + 1)
                    search(k, qt // KT, qt % KT, j)
                    k += 1
                if qt == KT:
                    pe.wait_ge(wide_read, k - WIDE + 1)
                    turn_shift(0, k)
                    k += 1
            bodies(pe, slot_work)
            pe.wait_ge(wide_read, base(SLOTS))
            turn_o(SLOTS - 1, 0)


def stage_c(nc, x, out, o_sb, ffn_sb, ident_sb, wout_sb, bout_row):
    BUFS = 4
    with ExitStack() as ctx:
        def sb(name, shape, dt=F32):
            return ctx.enter_context(nc.sbuf_tensor(name, shape, dt))

        def sem(name):
            return ctx.enter_context(nc.semaphore(name))

        x_sb = [sb(f"xc_sb{i}", [P, D]) for i in range(BUFS)]
        o_tile = [sb(f"o_tile{i}", [P, D]) for i in range(2)]
        ot_sb = [sb(f"ot_sb{i}", [P, D]) for i in range(2)]
        part_sum = [sb(f"part_sum{i}", [P, D]) for i in range(2)]
        y_sb = [sb(f"y_sb{i}", [P, D]) for i in range(BUFS)]
        ot_ps = [ctx.enter_context(nc.psum_tensor(f"ot_ps{i}", [P, D], F32)) for i in range(2)]
        y_ps = [ctx.enter_context(nc.psum_tensor(f"y_ps{i}", [P, 512], F32)) for i in range(2)]
        x_in = [sem(f"xc_in{i}") for i in range(BUFS)]
        y_out = [sem(f"y_out{i}") for i in range(BUFS)]
        tile_done = sem("tile_done")
        ot_mm = sem("ot_mm")
        ot_done = sem("ot_done")
        y_mm = sem("y_mm")
        sum_done = sem("sum_done")
        xb_done = sem("xb_done")
        y_done = sem("y_done")
        x_rows = x.rearrange("b (t p) d -> (b t) p d", p=P)
        out_rows = out.rearrange("b (t p) d -> (b t) p d", p=P)
        CC = KT // QC
        block = ctx.enter_context(nc.Block())

        @block.sync
        def _(sp):
            for c in range(BUFS):
                sp.sem_inc(y_out[c], 16)

            def load(n, c):
                sp.dma_start(x_sb[c][:], x_rows[bass.ds(n, 1)].rearrange("a p d -> (a p) d")).then_inc(x_in[c], 16)

            def store(n, c):
                sp.wait_ge(y_done, n + BUFS + 1)
                sp.dma_start(out_rows[bass.ds(n, 1)].rearrange("a p d -> (a p) d"), y_sb[c][:]).then_inc(y_out[c], 16)

            for c in range(BUFS):
                load(c, c)
            with sp.Fori(0, TILES // BUFS - 1) as i:
                for c in range(BUFS):
                    store(i * BUFS + c, c)
                    load(i * BUFS + BUFS + c, c)
            for c in range(BUFS):
                store(TILES - BUFS + c, c)
            for c in range(BUFS):
                sp.wait_ge(y_out[c], 16 * (1 + TILES // BUFS))

        @block.scalar
        def _(act):
            act.sem_inc(ot_done, 2)
            with act.Fori(0, TILES // BUFS) as i:
                for c in range(BUFS):
                    n = i * BUFS + c
                    act.wait_ge(ot_mm, n + 3)
                    act.wait_ge(y_mm, n + 1)
                    nc.scalar.copy(ot_sb[c % 2][:], ot_ps[c % 2][:]).then_inc(ot_done, 1)

        @block.gpsimd
        def _(pool):
            pool.sem_inc(xb_done, BUFS)
            with pool.Fori(0, B) as b:
                with pool.Fori(0, QC) as q:
                    for c in range(CC):
                        n = (b * QC + q) * CC + c
                        pool.wait_ge(ot_mm, n + 1)
                        nc.gpsimd.tensor_copy(o_tile[c % 2][:].rearrange("p (h a d) -> p h a d", a=1, d=DH),
                                              o_sb[:, bass.ds(b * H, H), bass.ds(q + c * QC, 1), :]).then_inc(tile_done, 1)
                        pool.wait_ge(x_in[c], (b * QC + q) * 16 + 16)
                        nc.gpsimd.tensor_tensor(x_sb[c][:], x_sb[c][:], bout_row[:], ALU.add).then_inc(xb_done, 1)

        @block.tensor
        def _(pe):
            pe.sem_inc(ot_mm, 2)
            pe.sem_inc(y_mm, 2)

            def turn(n, c):
                pe.wait_ge(tile_done, n + 1)
                pe.wait_ge(ot_done, n + 1)
                for k in range(KD):
                    last = nc.tensor.transpose(ot_ps[c % 2][:, k * P:(k + 1) * P], o_tile[c % 2][:, k * P:(k + 1) * P], ident_sb[:])
                last.then_inc(ot_mm, 1)

            def project(n, c):
                pe.wait_ge(ot_done, n + 3)
                pe.wait_ge(sum_done, n + 1)
                for k in range(KD):
                    last = nc.tensor.matmul(y_ps[c % 2][:, 0:D], ot_sb[c % 2][:, k * P:(k + 1) * P], wout_sb[:, k, :],
                                            start=(k == 0), stop=(k == KD - 1))
                last.then_inc(y_mm, 1)

            turn(0, 0)
            with pe.Fori(0, TILES // BUFS - 1) as i:
                for c in range(BUFS):
                    turn(i * BUFS + c + 1, c + 1)
                    project(i * BUFS + c, c)
            for c in range(BUFS):
                if c + 1 < BUFS:
                    turn(TILES - BUFS + c + 1, c + 1)
                project(TILES - BUFS + c, c)

        @block.vector
        def _(dve):
            dve.sem_inc(sum_done, 2)
            dve.sem_inc(y_done, BUFS)
            with dve.Fori(0, TILES // BUFS) as i:
                for c in range(BUFS):
                    n = i * BUFS + c
                    dve.wait_ge(y_mm, n + 3)
                    dve.wait_ge(y_done, n + 3)
                    nc.vector.tensor_tensor(part_sum[c % 2][:], y_ps[c % 2][:, 0:D],
                                            ffn_sb[:, bass.ds(n, 1), :].rearrange("p a d -> p (a d)"), ALU.add).then_inc(sum_done, 1)
                    dve.wait_ge(sum_done, n + 3)
                    dve.wait_ge(xb_done, n + BUFS + 1)
                    dve.wait_ge(y_out[c], i * 16 + 16)
                    nc.vector.tensor_tensor(y_sb[c][:], part_sum[c % 2][:], x_sb[c][:], ALU.add).then_inc(y_done, 1)


_INS = ["L0_attn_x", "L0_attn_w_qkv", "L0_attn_b_qkv", "L0_attn_w_out", "L0_attn_b_out", "L0_ffn_tile_sigs", "L0_ffn_W",
        "L0_ffn_b"]


def kernel(**inputs):
    import numpy as _np
    import concourse.bacc as _bacc
    from concourse import mybir as _mybir
    from concourse.bass_utils import run_bass_kernel_spmd as _run

    nc = _bacc.Bacc("TRN2", target_bir_lowering=False, num_devices=1)
    arrays, args = {}, []

    def give(name, a):
        a = _np.ascontiguousarray(a)
        arrays[name] = a
        args.append(nc.dram_tensor(name, a.shape, _mybir.dt.from_np(a.dtype), kind="ExternalInput").ap())

    for name in _INS:
        give(f"in_{name}_dram", inputs[name].T if name == "L0_ffn_tile_sigs" else inputs[name])
    give("in_bqk_cols_dram", _np.asarray(inputs["L0_attn_b_qkv"])[0:2 * D].reshape(MB, P).T)
    for name, a in zip(("rope", "ident", "swap", "pick", "rank"), build_tables()):
        give(f"table_{name}_dram", a)
    out = nc.dram_tensor("out_dram", (B, L, D), _mybir.dt.float32, kind="ExternalOutput").ap()
    routed_attention_kernel(nc, *args, out)
    r = _run(nc, [arrays], core_ids=[0])
    return r.results[0]["out_dram"]
```

```python
from contextlib import ExitStack

import numpy as np

import concourse.bass as bass
from concourse import mybir

ALU = mybir.AluOpType
ACT = mybir.ActivationFunctionType
F32 = mybir.dt.float32
BF16 = mybir.dt.bfloat16
I32 = mybir.dt.int32
AX_X = mybir.AxisListType.X

P = 128
B, L, D = 2, 2048, 256
H = 16
DH = D // H
T = 8
THETA = 500.0
EPS = 1e-5

TOKENS = B * L
TILES = TOKENS // P
KD = D // P
GROUP = 512
GT = GROUP // P
GROUPS = L // GROUP
MB = 2 * KD
PARTS = 3

SLOTS = B * H
KT = L // P
QC = L // 512
HEAD_BUFS = 4
WIDE = 3
EARLY = 2
LEAD = 5
P_BUFS = 3
RS = 6 * DH
PAIRS = ((0, 0), (0, 1), (0, 2), (1, 0), (1, 1), (2, 0))
RA = RS + PARTS
LOG_P = P.bit_length() - 1
VW = 32

NT = TILES + T
FFN_TILES = (2, 2, 1, 1)
BODY_TILES = sum(FFN_TILES)


def build_tables():
    half = DH // 2
    freqs = (1.0 / np.float32(THETA) ** (np.arange(half, dtype=np.float32) / np.float32(half)))
    freqs = freqs.astype(np.float32)
    angles = np.arange(L, dtype=np.float32)[None, :] * freqs[:, None]
    cos, sin = np.cos(angles), np.sin(angles)
    heads = P // DH
    rope = np.stack([np.tile(np.concatenate([cos, cos]), (heads, 1)),
                     np.tile(np.concatenate([-sin, sin]), (heads, 1))]).astype(np.float32)
    ident = np.eye(P, dtype=np.float32)
    swap = np.zeros((P, P), np.float32)
    for m in range(P):
        head, d = divmod(m, DH)
        swap[head * DH + (d + half) % DH, m] = 1.0
    rank = np.arange(T, 0, -1, dtype=np.float32)[None, :]
    p = np.arange(P, dtype=np.float32)[:, None]
    before = (p < p.T).astype(np.float32)
    upto = np.tril(np.ones((T, T), np.float32)).reshape(1, -1).repeat(P, 0)
    tile_row = (P * np.arange(NT, dtype=np.float32))[None, :].repeat(P, 0)
    dispatch = np.concatenate([before, upto, tile_row, p], 1)
    token_id = (np.arange(P)[:, None] + P * np.arange(TILES)[None, :]).astype(np.int32)
    return rope, ident, swap, rank, dispatch, token_id


def routed_attention_kernel(nc, x, w_qkv, b_qkv, w_out, b_out, sigs_t, ffn_w, ffn_b,
                            bqk_cols, rope, ident, swap, rank, dispatch, token_id, out):
    parts_dram = nc.dram_tensor("qk_parts", (PARTS, 2 * D, TOKENS), BF16, kind="Internal").ap()
    xn_dram = nc.dram_tensor("xn", (TOKENS, D), F32, kind="Internal").ap()
    id_dram = nc.dram_tensor("token_of_row", (NT * P, 1), I32, kind="Internal").ap()
    y_dram = nc.dram_tensor("ffn_sorted", (NT * P, D), F32, kind="Internal").ap()

    with ExitStack() as top:
        def keep(name, shape, dt=F32):
            return top.enter_context(nc.sbuf_tensor(name, shape, dt))

        v_sb = keep("v_sb", [P, TILES, D])
        q_st = [keep(f"q_st{i}", [P, L], BF16) for i in range(HEAD_BUFS)]
        k_st = [keep(f"k_st{i}", [P, L], BF16) for i in range(HEAD_BUFS)]
        stack_in = [top.enter_context(nc.semaphore(f"stack_in{i}")) for i in range(HEAD_BUFS)]
        chunk_max = [keep(f"chunk_max{i}", [P, KT, QC]) for i in range(2)]
        vh = [keep(f"vh{i}", [P, KT, VW]) for i in range(HEAD_BUFS)]
        shift = keep("shift", [P, P], BF16)
        ones = keep("ones", [P, P], BF16)
        before = keep("before", [P, P], BF16)
        onehot = keep("onehot", [P, TILES + 1, T], BF16)
        ident_sb = keep("ident_sb", [P, P])
        wout_sb = keep("wout_sb", [P, KD, D])
        bout_row = keep("bout_row", [P, D])
        dispatch_sb = keep("dispatch_sb", [P, P + T * T + NT + 1])
        id_sb = keep("id_sb", [P, TILES], I32)
        ident_bf = keep("ident_bf", [P, P], BF16)

        stage_a(nc, x, w_qkv, b_qkv, w_out, b_out, sigs_t, bqk_cols, rope, ident, swap, rank, dispatch, token_id,
                parts_dram, xn_dram, v_sb, onehot, ident_sb, ident_bf, wout_sb, bout_row, dispatch_sb, id_sb,
                q_st, k_st, stack_in, vh, shift, ones, before, chunk_max)
        ffn_sb = keep("ffn_sb", [P, TILES, D])
        o_sb = keep("o_sb", [P, KT, SLOTS * DH])
        stage_b(nc, ffn_w, ffn_b, parts_dram, xn_dram, id_dram, y_dram, v_sb, ffn_sb, o_sb, onehot, ident_sb, ident_bf,
                dispatch_sb, id_sb, q_st, k_st, stack_in, vh, shift, ones, before, chunk_max)
        stage_c(nc, x, out, o_sb, ffn_sb, ident_sb, wout_sb, bout_row)


def load_stacks(sp, parts_dram, q_st, k_st, signal, row, cols):
    for r, (qa, ka) in enumerate(PAIRS):
        sp.dma_start(q_st[r * DH:(r + 1) * DH, :], parts_dram[qa, bass.ds(row, DH), cols]).then_inc(signal, 16)
        sp.dma_start(k_st[r * DH:(r + 1) * DH, :], parts_dram[ka, bass.ds(row + D, DH), cols]).then_inc(signal, 16)


def stage_a(nc, x, w_qkv, b_qkv, w_out, b_out, sigs_t, bqk_cols, rope, ident, swap, rank, dispatch, token_id,
            parts_dram, xn_dram, v_sb, onehot, ident_sb, ident_bf, wout_sb, bout_row, dispatch_sb, id_sb,
            q_st, k_st, stack_in, vh, shift, ones, before, chunk_max):
    BODY = 2 * MB
    BODIES = B * GROUPS // 2
    LATE = 2 * (B - 1) + 4
    DRAIN = 4
    VN = D + T
    with ExitStack() as ctx:
        def sb(name, shape, dt=F32):
            return ctx.enter_context(nc.sbuf_tensor(name, shape, dt))

        def sem(name):
            return ctx.enter_context(nc.semaphore(name))

        wqk_sb = sb("wqk_sb", [P, KD, 2 * D])
        wvs_sb = sb("wvs_sb", [P, KD, VN])
        sig_sb = sb("sig_sb", [P, KD, T])
        sneg = sb("sneg", [P, KD, T])
        spos = sb("spos", [P, KD, T])
        swap_sb = sb("swap_sb", [P, P])
        cos_sb = sb("cos_sb", [P, TOKENS])
        sin_sb = sb("sin_sb", [P, TOKENS])
        bqk_raw = sb("bqk_raw", [P, MB])
        bqk = sb("bqk", [P, MB])
        bv_row = sb("bv_row", [P, D])
        rank_row = sb("rank_row", [P, T])
        eps_col = sb("eps_col", [P, 1])
        spare = sb("spare", [P, 1])
        x_sb = [sb(f"x_sb{i}", [P, GT, D]) for i in range(2)]
        xn_sb = [sb(f"xn_sb{i}", [P, GT, D]) for i in range(2)]
        xt_sb = [sb(f"xt_sb{i}", [P, KD, GROUP]) for i in range(2)]
        stats = sb("stats", [P, GT, 6])
        count_seen = sb("count_seen", [P, 1])
        moments = sb("moments", [P, GT, 2])
        std = sb("std", [P, GT])
        rstd = sb("rstd", [P, GT])
        gate = sb("gate", [P, GT, T])
        gmax = sb("gmax", [P, GT])
        ranked = sb("ranked", [P, GT, T])
        first = sb("first", [P, GT])
        qk_sb = [sb(f"qk_sb{i}", [P, GROUP]) for i in range(2)]
        qcos = [sb(f"qcos{i}", [P, GROUP]) for i in range(2)]
        qsin = [sb(f"qsin{i}", [P, GROUP]) for i in range(2)]
        roped = [sb(f"roped{i}", [P, GROUP]) for i in range(2)]
        rest = [sb(f"rest{i}", [P, GROUP]) for i in range(4)]
        parts = [sb(f"parts{i}", [P, PARTS, MB, GROUP], BF16) for i in range(2)]

        xt_ps = [ctx.enter_context(nc.psum_tensor(f"xt_ps{k}", [P, GROUP], F32)) for k in range(KD)]
        qk_ps = [ctx.enter_context(nc.psum_tensor(f"qk_ps{k}", [P, GROUP], F32)) for k in range(2)]
        sw_ps = [ctx.enter_context(nc.psum_tensor(f"sw_ps{k}", [P, GROUP], F32)) for k in range(2)]
        v_ps = [ctx.enter_context(nc.psum_tensor(f"v_ps{k}", [P, 512], F32)) for k in range(2)]

        norm_in = sem("norm_in")
        weights_in = sem("weights_in")
        small_in = sem("small_in")
        tables_in = sem("tables_in")
        late_in = sem("late_in")
        more_tables_in = sem("more_tables_in")
        early_mm = sem("early_mm")
        early_read = sem("early_read")
        vh_zero = sem("vh_zero")
        const_rows = sem("const_rows")
        x_in = [sem(f"x_in{i}") for i in range(2)]
        consts_done = sem("consts_done")
        signs_done = sem("signs_done")
        stats_done = sem("stats_done")
        moments_done = sem("moments_done")
        std_done = sem("std_done")
        rstd_done = sem("rstd_done")
        xn_done = sem("xn_done")
        xt_mm = sem("xt_mm")
        xt_done = sem("xt_done")
        qk_mm = sem("qk_mm")
        qk_done = sem("qk_done")
        v_mm = sem("v_mm")
        v_done = sem("v_done")
        gate_step = sem("gate_step")
        swap_mm = sem("swap_mm")
        qk_seen = sem("qk_seen")
        qcos_done = sem("qcos_done")
        qsin_done = sem("qsin_done")
        roped_done = sem("roped_done")
        hi_done = sem("hi_done")
        rest_done = sem("rest_done")
        mid_done = sem("mid_done")
        xn_out = [sem(f"xn_out{i}") for i in range(2)]
        parts_out = [sem(f"parts_out{i}") for i in range(2)]
        lo_done = sem("lo_done")

        x_view = x.rearrange("b (g t p) d -> (b g) p t d", t=GT, p=P)
        xn_view = xn_dram.rearrange("(g t p) d -> g p t d", t=GT, p=P)
        block = ctx.enter_context(nc.Block())

        def exists(i, s):
            return not isinstance(i, int) or 0 <= i * BODY + s < BODIES * BODY

        def later(G, n):
            return not isinstance(G, int) or G >= n

        def known_group(G, s, n):
            return isinstance(G, int) and G == n and s % MB == 0

        def group_exists(i, s):
            return exists(i, s // MB * MB)

        def group(i, s):
            return i * 2 + s // MB

        def bodies(engine, step):
            for s in range(BODY):
                step(0, s)
            with engine.Fori(1, BODIES - 1) as i:
                for s in range(BODY):
                    step(i, s)
            for s in range(BODY + DRAIN):
                step(BODIES - 1, s)

        def rows(view, G):
            return view[bass.ds(G, 1)].rearrange("a p t d -> (a p) t d")

        @block.sync
        def _(sp):
            def const(to, of, signal):
                sp.dma_start(to, of).then_inc(signal, 16)

            def step(i, s):
                if s % MB or not exists(i, s):
                    return
                G, g = group(i, s), s // MB % 2
                if isinstance(G, int) and G == 2 * BODIES - 2:
                    for k in range(2):
                        sp.wait_ge(parts_out[k], 16 * PARTS * GROUPS // 2)
                    load_stacks(sp, parts_dram, q_st[0], k_st[0], stack_in[0], 0, slice(0, L))
                sp.wait_ge(xn_done, G + 1)
                sp.dma_start(rows(xn_view, G), xn_sb[g][:]).then_inc(xn_out[g], 16)
                for a, done, credits in ((0, hi_done, 0), (1, mid_done, 0), (2, lo_done, 4)):
                    sp.wait_ge(done, (G + 1) * MB + credits)
                    sp.dma_start(parts_dram[a].rearrange("(m p) n -> p m n", p=P)[:, :, bass.ds(G * GROUP, GROUP)],
                                 parts[g][:, a]).then_inc(parts_out[g], 16)

            sp.dma_start(x_sb[0][:], rows(x_view, 0)).then_inc(x_in[0], 16)
            const(ident_sb[:], ident, norm_in)
            const(wqk_sb[:], w_qkv[:, 0:2 * D].rearrange("(k p) n -> p k n", p=P), weights_in)
            sp.dma_start(x_sb[1][:], rows(x_view, 1)).then_inc(x_in[1], 16)
            const(cos_sb[:, 0:GROUP], rope[0, :, 0:GROUP], tables_in)
            bodies(sp, step)
            for g in range(2):
                sp.wait_ge(xn_out[g], 16 * BODIES)
                sp.wait_ge(parts_out[g], 16 * PARTS * BODIES)

        @block.scalar
        def _(act):
            act.wait_ge(consts_done, 1)
            nc.scalar.activation(spare[:], eps_col[:], ACT.Sqrt)
            act.dma_start(bqk_raw[:], bqk_cols).then_inc(small_in, 16)
            act.dma_start(sig_sb[:], sigs_t.rearrange("(k p) t -> p k t", p=P)).then_inc(small_in, 16)
            act.dma_start(wvs_sb[:, :, 0:D], w_qkv[:, 2 * D:3 * D].rearrange("(k p) n -> p k n", p=P)).then_inc(small_in, 16)
            act.dma_start(swap_sb[:], swap).then_inc(small_in, 16)
            act.dma_start(bv_row[:], b_qkv[2 * D:3 * D].partition_broadcast(P)).then_inc(small_in, 16)
            act.dma_start(rank_row[:], rank[0, :].partition_broadcast(P)).then_inc(small_in, 16)
            act.dma_start(sin_sb[:, 0:GROUP], rope[1, :, 0:GROUP]).then_inc(tables_in, 16)

            def load_x(i, s):
                G, g = group(i, s), s // MB % 2
                act.wait_ge(xn_done, G - 1)
                act.dma_start(x_sb[g][:], rows(x_view, G)).then_inc(x_in[g], 16)

            def std_dev(i, s):
                act.wait_ge(moments_done, group(i, s) + 1)
                nc.scalar.activation(std[:], moments[:, :, 1], ACT.Sqrt, bias=eps_col[:]).then_inc(std_done, 1)

            def copy_xt(i, s):
                G, g = group(i, s), s // MB % 2
                act.wait_ge(xt_mm, G + 1)
                if later(G, 2):
                    act.wait_ge(v_mm, (G - 1) * GT)
                for k in range(KD):
                    last = nc.scalar.copy(xt_sb[g][:, k, :], xt_ps[k][:])
                last.then_inc(xt_done, 1)

            def add_bias(i, s):
                n, m = i * BODY + s, s % MB
                act.wait_ge(qk_mm, n + 1)
                act.wait_ge(swap_mm, n + 1)
                act.wait_ge(qcos_done, n + 1)
                nc.scalar.activation(qk_sb[s % 2][:], qk_ps[s % 2][:], ACT.Identity, bias=bqk[:, m:m + 1],
                                     scale=1.0 if m < KD else float(DH) ** -0.5).then_inc(qk_done, 1)

            def hi_part(i, s):
                G, g, m = group(i, s), s // MB % 2, s % MB
                act.wait_ge(roped_done, i * BODY + s + 3)
                if m == 0 and later(G, 2):
                    act.wait_ge(parts_out[g], (i + s // BODY) * 16 * PARTS)
                nc.scalar.copy(parts[g][:, 0, m, :], roped[s % 2][:]).then_inc(hi_done, 1)

            def mid_part(i, s):
                g, m = s // MB % 2, s % MB
                act.wait_ge(rest_done, i * BODY + s + 3)
                nc.scalar.copy(parts[g][:, 1, m, :], rest[s % 4][:]).then_inc(mid_done, 1)

            def step(i, s):
                if exists(i, s):
                    add_bias(i, s)
                if s % MB == 0 and group_exists(i, s + 2 * MB):
                    load_x(i, s + 2 * MB)
                if s % MB == 3 and group_exists(i, s + MB):
                    copy_xt(i, s + MB)
                if exists(i, s - 2):
                    hi_part(i, s - 2)
                if exists(i, s - 3):
                    mid_part(i, s - 3)
                if s % MB == 0 and group_exists(i, s + MB):
                    std_dev(i, s + MB)

            std_dev(0, 0)
            copy_xt(0, 0)
            act.wait_ge(consts_done, 3)
            bodies(act, step)

        @block.gpsimd
        def _(pool):
            pool.sem_inc(qcos_done, 2)
            pool.sem_inc(rest_done, 2)
            for n in range(HEAD_BUFS):
                pool.memset(vh[n][:], 0.0).then_inc(vh_zero, 1)
            pool.memset(shift[:], 0.0).then_inc(const_rows, 1)
            pool.memset(ones[:], 1.0).then_inc(const_rows, 1)
            pool.wait_ge(const_rows, 2)
            for n in range(HEAD_BUFS):
                pool.memset(k_st[n][RS:RA, :], 1.0).then_inc(const_rows, 1)
                pool.wait_ge(const_rows, 3 + n)
            pool.wait_ge(vh_zero, HEAD_BUFS)
            for n in range(HEAD_BUFS):
                pool.memset(vh[n][:, :, DH:DH + 1], 1.0)
            pool.wait_ge(weights_in, 16)
            pool.wait_ge(small_in, 16 * 6)
            for n, table in enumerate((cos_sb, sin_sb)):
                pool.dma_start(table[:, GROUP:L], rope[n, :, GROUP:L]).then_inc(more_tables_in, 16)
            for b in range(1, B):
                pool.dma_start(cos_sb[:, b * L:(b + 1) * L], rope[0]).then_inc(late_in, 16)
                pool.dma_start(sin_sb[:, b * L:(b + 1) * L], rope[1]).then_inc(late_in, 16)
            pool.dma_start(wout_sb[:], w_out.rearrange("(k p) n -> p k n", p=P)).then_inc(late_in, 16)
            pool.dma_start(bout_row[:], b_out.partition_broadcast(P)).then_inc(late_in, 16)
            pool.dma_start(dispatch_sb[:], dispatch).then_inc(late_in, 16)
            pool.dma_start(id_sb[:], token_id).then_inc(late_in, 16)
            pool.wait_ge(tables_in, 32)

            def cos_product(i, s):
                n, G = i * BODY + s, group(i, s)
                if known_group(G, s, 1):
                    pool.wait_ge(more_tables_in, 32)
                if s == 0 and not isinstance(i, int):
                    pool.wait_ge(late_in, 16 * LATE)
                pool.wait_ge(qk_done, n + 1)
                pool.wait_ge(roped_done, n + 1)
                pool.sem_inc(qk_seen, 1)
                nc.gpsimd.tensor_tensor(qcos[s % 2][:], qk_sb[s % 2][:], cos_sb[:, bass.ds(G * GROUP, GROUP)],
                                        ALU.mult).then_inc(qcos_done, 1)

            def less_hi(i, s):
                n, g, m = i * BODY + s, s // MB % 2, s % MB
                pool.wait_ge(hi_done, n + 1)
                pool.wait_ge(lo_done, n + 1)
                nc.gpsimd.tensor_tensor(rest[s % 4][:], roped[s % 2][:], parts[g][:, 0, m, :],
                                        ALU.subtract).then_inc(rest_done, 1)

            def step(i, s):
                if exists(i, s):
                    cos_product(i, s)
                if exists(i, s - 2):
                    less_hi(i, s - 2)

            bodies(pool, step)

        @block.vector
        def _(dve):
            dve.sem_inc(roped_done, 2)
            dve.sem_inc(qsin_done, 2)
            dve.sem_inc(lo_done, 4)
            dve.sem_inc(v_done, 2)
            dve.memset(eps_col[:], EPS).then_inc(consts_done, 1)
            dve.memset(onehot[:, TILES:TILES + 1, :], 0.0)

            def norm(i, s):
                G, g = group(i, s), s // MB % 2
                dve.wait_ge(x_in[g], (i + s // BODY) * 16 + 16)
                for t in range(GT):
                    last = nc.vector.bn_stats(stats[:, t, :], x_sb[g][:, t, :])
                last.then_inc(stats_done, 1)
                dve.wait_ge(stats_done, G + 1)
                nc.vector.tensor_copy(count_seen[:], stats[:, 0, 0:1])
                for t in range(GT):
                    last = nc.vector.bn_aggr(moments[:, t, :], stats[:, t, :])
                last.then_inc(moments_done, 1)

            def norm_rest(i, s):
                G, g = group(i, s), s // MB % 2
                dve.wait_ge(std_done, G + 1)
                nc.vector.reciprocal(rstd[:], std[:]).then_inc(rstd_done, 1)
                dve.wait_ge(rstd_done, G + 1)
                if later(G, 2):
                    dve.wait_ge(xt_mm, G - 1)
                    dve.wait_ge(xn_out[g], (i + s // BODY) * 16)
                for t in range(GT):
                    last = nc.vector.tensor_scalar(xn_sb[g][:, t, :], x_sb[g][:, t, :], moments[:, t, 0:1],
                                                   rstd[:, t:t + 1], ALU.subtract, ALU.mult)
                last.then_inc(xn_done, 1)

            def take_v(i, s):
                n, t = i * BODY + s, s % GT
                dve.wait_ge(v_mm, n + 1)
                nc.vector.tensor_tensor(v_sb[:, bass.ds(n, 1), :].rearrange("p a d -> p (a d)"), v_ps[s % 2][:, 0:D],
                                        bv_row[:], ALU.add)
                nc.vector.tensor_copy(gate[:, t, :], v_ps[s % 2][:, D:VN]).then_inc(v_done, 1)

            def route(i, s):
                G = group(i, s)
                dve.wait_ge(v_done, (G + 1) * GT + 2)
                nc.vector.tensor_reduce(gmax[:], gate[:], AX_X, ALU.max).then_inc(gate_step, 1)
                dve.wait_ge(gate_step, G * 4 + 1)
                for t in range(GT):
                    last = nc.vector.scalar_tensor_tensor(ranked[:, t, :], gate[:, t, :], gmax[:, t:t + 1], rank_row[:],
                                                          ALU.is_equal, ALU.mult)
                last.then_inc(gate_step, 1)
                dve.wait_ge(gate_step, G * 4 + 2)
                nc.vector.tensor_reduce(first[:], ranked[:], AX_X, ALU.max).then_inc(gate_step, 1)
                dve.wait_ge(gate_step, G * 4 + 3)
                for t in range(GT):
                    last = nc.vector.tensor_scalar(onehot[:, bass.ds(G * GT + t, 1), :].rearrange("p a e -> p (a e)"),
                                                   rank_row[:], first[:, t:t + 1], None, ALU.is_equal)
                last.then_inc(gate_step, 1)

            def rope_sum(i, s):
                n, G = i * BODY + s, group(i, s)
                if known_group(G, s, 1):
                    dve.wait_ge(more_tables_in, 32)
                if s == 0 and not isinstance(i, int):
                    dve.wait_ge(late_in, 16 * LATE)
                dve.wait_ge(swap_mm, n + 3)
                dve.wait_ge(roped_done, n + 1)
                nc.vector.tensor_tensor(qsin[s % 2][:], sw_ps[s % 2][:], sin_sb[:, bass.ds(G * GROUP, GROUP)],
                                        ALU.mult).then_inc(qsin_done, 1)
                dve.wait_ge(qcos_done, n + 3)
                dve.wait_ge(qsin_done, n + 3)
                dve.wait_ge(rest_done, n + 1)
                nc.vector.tensor_tensor(roped[s % 2][:], qcos[s % 2][:], qsin[s % 2][:], ALU.add).then_inc(roped_done, 1)

            def lo_part(i, s):
                n, g, m = i * BODY + s, s // MB % 2, s % MB
                dve.wait_ge(rest_done, n + 3)
                dve.wait_ge(mid_done, n + 1)
                nc.vector.tensor_tensor(parts[g][:, 2, m, :], rest[s % 4][:], parts[g][:, 1, m, :],
                                        ALU.subtract).then_inc(lo_done, 1)

            def step(i, s):
                if s % MB == 0 and group_exists(i, s + MB):
                    norm(i, s + MB)
                if s % MB == 1 and exists(i, s - MB):
                    route(i, s - MB)
                if exists(i, s - 1):
                    take_v(i, s - 1)
                    rope_sum(i, s - 1)
                if exists(i, s - 4):
                    lo_part(i, s - 4)
                if s % MB == 1 and group_exists(i, s + MB):
                    norm_rest(i, s + MB)

            norm(0, 0)
            norm_rest(0, 0)
            dve.wait_ge(small_in, 16 * 6)
            nc.vector.tensor_scalar(spos[:], sig_sb[:], 0.0, None, ALU.is_gt).then_inc(signs_done, 1)
            nc.vector.tensor_scalar(sneg[:], sig_sb[:], 0.0, None, ALU.is_lt).then_inc(signs_done, 1)
            nc.vector.tensor_copy(bqk[:, 0:KD], bqk_raw[:, 0:KD]).then_inc(consts_done, 1)
            nc.vector.tensor_scalar(bqk[:, KD:MB], bqk_raw[:, KD:MB], float(DH) ** -0.5, None, ALU.mult).then_inc(consts_done, 1)
            dve.wait_ge(signs_done, 2)
            nc.vector.tensor_tensor(wvs_sb[:, :, D:VN], spos[:], sneg[:], ALU.subtract).then_inc(signs_done, 1)
            dve.wait_ge(norm_in, 16)
            nc.vector.tensor_copy(ident_bf[:], ident_sb[:])
            dve.wait_ge(tables_in, 32)
            bodies(dve, step)
            for r in range(EARLY * QC):
                qt, j = divmod(r, QC)
                dve.wait_ge(early_mm, r + 1)
                nc.vector.tensor_reduce(chunk_max[0][:, qt, j:j + 1], xt_ps[r % KD][:], AX_X, ALU.max).then_inc(early_read, 1)
            nc.vector.tensor_copy(before[:], dispatch_sb[:, 0:P])

        @block.tensor
        def _(pe):
            pe.sem_inc(swap_mm, 2)

            def transposes(i, s):
                G, g = group(i, s), s // MB % 2
                pe.wait_ge(xn_done, G + 1)
                if later(G, 1):
                    pe.wait_ge(xt_done, G)
                for k in range(KD):
                    for t in range(GT):
                        last = nc.tensor.transpose(xt_ps[k][:, t * P:(t + 1) * P], xn_sb[g][:, t, k * P:(k + 1) * P],
                                                   ident_sb[:])
                last.then_inc(xt_mm, 1)

            def project(i, s):
                g, m = s // MB % 2, s % MB
                if m == 0:
                    pe.wait_ge(xt_done, group(i, s) + 1)
                if exists(i, s - 2):
                    pe.wait_ge(qk_done, i * BODY + s - 1)
                for k in range(KD):
                    last = nc.tensor.matmul(qk_ps[s % 2][:], wqk_sb[:, k, m * P:(m + 1) * P], xt_sb[g][:, k, :],
                                            start=(k == 0), stop=(k == KD - 1))
                last.then_inc(qk_mm, 1)

            def project_v(i, s):
                g, t = s // MB % 2, s % GT
                if isinstance(i, int) and i * BODY + s == 0:
                    pe.wait_ge(small_in, 16 * 6)
                    pe.wait_ge(signs_done, 3)
                pe.wait_ge(v_done, i * BODY + s + 1)
                for k in range(KD):
                    last = nc.tensor.matmul(v_ps[s % 2][:, 0:VN], xt_sb[g][:, k, t * P:(t + 1) * P], wvs_sb[:, k, :],
                                            start=(k == 0), stop=(k == KD - 1))
                last.then_inc(v_mm, 1)

            def swap_halves(i, s):
                pe.wait_ge(qk_done, i * BODY + s + 1)
                pe.wait_ge(qsin_done, i * BODY + s + 1)
                nc.tensor.matmul(sw_ps[s % 2][:], swap_sb[:], qk_sb[s % 2][:], start=True, stop=True).then_inc(swap_mm, 1)

            def step(i, s):
                if exists(i, s):
                    project(i, s)
                if s % MB == MB - 1 and group_exists(i, s + MB):
                    transposes(i, s + MB)
                if exists(i, s - 1):
                    project_v(i, s - 1)
                    swap_halves(i, s - 1)

            pe.wait_ge(norm_in, 16)
            transposes(0, 0)
            pe.wait_ge(weights_in, 16)
            bodies(pe, step)
            pe.wait_ge(xt_done, B * GROUPS)
            pe.wait_ge(stack_in[0], 16 * 2 * len(PAIRS))
            for r in range(EARLY * QC):
                qt, j = divmod(r, QC)
                if r >= KD:
                    pe.wait_ge(early_read, r - KD + 1)
                nc.tensor.matmul(xt_ps[r % KD][:], q_st[0][0:RS, qt * P:(qt + 1) * P], k_st[0][0:RS, j * GROUP:(j + 1) * GROUP],
                                 start=True, stop=True).then_inc(early_mm, 1)


def stage_b(nc, ffn_w, ffn_b, parts_dram, xn_dram, id_dram, y_dram, v_sb, ffn_sb, o_sb, onehot, ident_sb, ident_bf,
            dispatch_sb, id_sb, q_st, k_st, stack_in, vh, shift, ones, before, chunk_max):
    SHIFT = PARTS * KT
    LOADS = 2 * len(PAIRS)
    FETCHES = 3
    FFN_TURN_AT = (3, 7)
    FFN_AT = (5, 9)
    O_AT = 2
    TURN_AT = KT - LEAD + 1
    FIRST_USES = (KT + LEAD - EARLY) * QC + 1
    BODIES = SLOTS // HEAD_BUFS
    PLACE_STEPS = 19
    COLS = (TILES + 1) * T
    with ExitStack() as ctx:
        def sb(name, shape, dt=F32):
            return ctx.enter_context(nc.sbuf_tensor(name, shape, dt))

        def psum(name, shape):
            return ctx.enter_context(nc.psum_tensor(name, shape, F32))

        def sem(name):
            return ctx.enter_context(nc.semaphore(name))

        xs = [sb(f"xs{i}", [P, D]) for i in range(BODY_TILES)]
        w_tile = [sb(f"w_tile{i}", [P, KD * D]) for i in range(BODY_TILES)]
        b_tile = [sb(f"b_tile{i}", [P, D]) for i in range(BODY_TILES)]
        idx = [sb(f"idx{i}", [P, FETCHES], I32) for i in range(BODY_TILES)]
        xs_t = [sb(f"xs_t{i}", [P, D]) for i in range(2)]
        y_tile = [sb(f"y_tile{i}", [P, D]) for i in range(2)]
        counts = sb("counts", [P, COLS])
        over = sb("over", [P, T], I32)
        tiles_of = sb("tiles_of", [P, T], I32)
        padded = sb("padded", [P, T])
        upto_rows = sb("upto_rows", [P, T, T])
        end_row = sb("end_row", [P, T])
        start_row = sb("start_row", [P, T])
        place = sb("place", [P, TILES, T])
        place_own = sb("place_own", [P, TILES, T])
        place_sum = sb("place_sum", [P, TILES])
        row_of = sb("row_of", [P, TILES], I32)
        past = sb("past", [P, NT, T])
        past_count = sb("past_count", [P, NT])
        expert = sb("expert", [P, NT])
        tile_of = sb("tile_of", [P, TILES], I32)
        id_place_part = sb("id_place_part", [P, TILES])
        id_place = sb("id_place", [P, TILES], I32)
        token_of = sb("token_of", [P, NT], I32)
        tile_idx = sb("tile_idx", [P, NT, 2], I32)
        no_ids = sb("no_ids", [P, NT], I32)
        probs = [sb(f"probs{i}", [P, L]) for i in range(P_BUFS)]
        neg_max = sb("neg_max", [P, KT])
        shift_rest = sb("shift_rest", [P, 2, KT])
        shift_rows = sb("shift_rows", [SHIFT, P], BF16)
        o_acc = sb("o_acc", [P, 512])
        spare = sb("spare_exp", [P, 1])
        rden = sb("rden", [P, KT])

        st_ps = [psum(f"st_ps{i}", [P, L // 2]) for i in range(2)]
        place_ps = st_ps[0]
        wide_ps = [psum(f"wide_ps{i}", [P, 512]) for i in range(WIDE)]
        o_ps = psum("o_ps", [P, 512])

        vh_done = sem("vh_done")
        shift_in = sem("shift_in")
        st_mm = sem("st_mm")
        exp_done = sem("exp_done")
        pv_mm = sem("pv_mm")
        o_read = sem("o_read")
        wide_mm = sem("wide_mm")
        wide_read = sem("wide_read")
        shift_step = sem("shift_step")
        shift_read = sem("shift_read")
        rden_done = sem("rden_done")
        place_mm = sem("place_mm")
        place_step = sem("place_step")
        ids_zero = sem("ids_zero")
        ids_zero_out = sem("ids_zero_out")
        ids_out = sem("ids_out")
        ids_in = sem("ids_in")
        idx_done = sem("idx_done")
        idx_seen = sem("idx_seen")
        fetch_in = [sem(f"fetch_in{i}") for i in range(BODY_TILES)]
        ffn_done = sem("ffn_done")
        y_stored = [sem(f"y_stored{i}") for i in range(2)]
        back_in = sem("back_in")
        block = ctx.enter_context(nc.Block())

        def target(kt):
            return 1 + (kt + LEAD) // KT, (kt + LEAD) % KT

        def bodies(engine, slot_work):
            for u in range(HEAD_BUFS):
                slot_work(u, 0, u)
            with engine.Fori(1, BODIES - 1) as i:
                for u in range(HEAD_BUFS):
                    slot_work(i * HEAD_BUFS + u, i, u)
            for u in range(HEAD_BUFS):
                slot_work(SLOTS - HEAD_BUFS + u, BODIES - 1, u)

        def known(slot, n):
            return isinstance(slot, int) and slot == n

        def searched(slot, kt):
            return not (isinstance(slot, int) and slot + target(kt)[0] >= SLOTS)

        def ffn_tiles(slot, i, u):
            if known(i, 0):
                return []
            tiles = [sum(FFN_TILES[:u]) + n for n in range(FFN_TILES[u])]
            return [c for c in tiles if not isinstance(i, int) or (i - 1) * BODY_TILES + c < NT]

        def uses_in(slot):
            i, u = divmod(slot, HEAD_BUFS)
            return (KT * QC + 2 + 2 * len(ffn_tiles(slot, i, u)) - (slot == 0) - (slot == SLOTS - 1)
                    - QC * sum(not searched(slot, kt) for kt in range(KT)))

        def base(slot, i, u):
            if isinstance(slot, int):
                return FIRST_USES + sum(uses_in(n) for n in range(slot))
            body_uses = sum(uses_in(HEAD_BUFS + n) for n in range(HEAD_BUFS))
            return i * body_uses + (base(HEAD_BUFS + u, 1, u) - body_uses)

        def free_at(slot, i, u, k):
            if k >= WIDE:
                return base(slot, i, u) + k - WIDE + 1
            if known(slot, 0):
                uses = FIRST_USES
            else:
                if not isinstance(slot, int) and u == 0:
                    return base(slot, i, u)
                uses = uses_in(slot - 1 if isinstance(slot, int) else HEAD_BUFS + u - 1)
            return base(slot, i, u) + max(m for m in range(uses) if m % WIDE == k) - uses + 1

        @block.sync
        def _(sp):
            def load_slot(b, h, slot, u):
                sp.wait_ge(o_read, slot - HEAD_BUFS + 1)
                row, cols = h * DH, slice(b * L, (b + 1) * L)
                load_stacks(sp, parts_dram, q_st[u], k_st[u], stack_in[u], row, cols)

            def store_ffn(m, c):
                t = m * BODY_TILES + c
                sp.wait_ge(ffn_done, t + 1 + BODY_TILES)
                rows = y_dram[t * P:(t + 1) * P, :] if isinstance(m, int) else y_view[bass.ds(t, 1)].rearrange("n p d -> (n p) d")
                sp.dma_start(rows, y_tile[c % 2][:]).then_inc(y_stored[c % 2], 16)

            def load_body(b, j, stores):
                for u in range(HEAD_BUFS):
                    load_slot(b, j * HEAD_BUFS + u, j * HEAD_BUFS + (b * H + u), u)
                    if stores is not None:
                        for c in range(sum(FFN_TILES[:u]), sum(FFN_TILES[:u + 1])):
                            store_ffn(stores, c)

            y_view = y_dram.rearrange("(n p) d -> n p d", p=P)
            for c in range(2):
                sp.sem_inc(y_stored[c], 16)
            for u in range(1, HEAD_BUFS):
                load_stacks(sp, parts_dram, q_st[u], k_st[u], stack_in[u], u * DH, slice(0, L))
            sp.wait_ge(ids_zero, 1)
            sp.dma_start(id_dram.rearrange("(p n) a -> p (n a)", p=P), no_ids[:]).then_inc(ids_zero_out, 16)
            sp.wait_ge(ids_out, 16 * TILES)
            sp.dma_start(token_of[:], id_dram.rearrange("(p n) a -> p (n a)", p=P)).then_inc(ids_in, 16)
            load_body(0, 1, None)
            with sp.Fori(2, H // HEAD_BUFS) as j:
                load_body(0, j, j - 2)
            with sp.Fori(0, H // HEAD_BUFS) as j:
                load_body(1, j, j + (H // HEAD_BUFS - 2))
            m = NT // BODY_TILES
            for c in range(NT % BODY_TILES):
                store_ffn(m, c)
            for c in range(2):
                sp.wait_ge(y_stored[c], 16 * (1 + NT // 2))

        @block.gpsimd
        def _(pool):
            pool.memset(no_ids[:], 0).then_inc(ids_zero, 1)

            def take_v(b, h, slot, u):
                if not known(slot, u):
                    pool.wait_ge(o_read, slot - HEAD_BUFS + 1)
                nc.gpsimd.tensor_copy(vh[u][:, :, 0:DH], v_sb[:, b * KT:(b + 1) * KT, bass.ds(h * DH, DH)]).then_inc(vh_done, 1)

            def fetch(m, c):
                t = m * BODY_TILES + c
                pool.wait_ge(ffn_done, t + 1)
                nc.gpsimd.tensor_copy(idx[c][:, 0:1], token_of[:, bass.ds(t, 1)])
                nc.gpsimd.tensor_copy(idx[c][:, 1:3], tile_idx[:, bass.ds(t, 1), :].rearrange("p a n -> p (a n)")).then_inc(idx_done, 1)
                pool.wait_ge(idx_done, t + 1)
                pool.sem_inc(idx_seen, 1)
                for n, (to, of) in enumerate(((xs[c], xn_dram), (w_tile[c], w_rows), (b_tile[c], ffn_b))):
                    nc.gpsimd.indirect_dma_start(to[:], None, of,
                                                 bass.IndirectOffsetOnAxis(idx[c][:, n:n + 1], 0)).then_inc(fetch_in[c], 16)

            def take_body(b, j, m):
                for u in range(HEAD_BUFS):
                    take_v(b, j * HEAD_BUFS + u, j * HEAD_BUFS + (b * H + u), u)
                    for c in range(sum(FFN_TILES[:u]), sum(FFN_TILES[:u + 1])):
                        if not isinstance(m, int) or m * BODY_TILES + c < NT:
                            fetch(m, c)

            w_rows = ffn_w.rearrange("t (p k) n -> (t p) (k n)", k=KD)
            for u in range(HEAD_BUFS):
                take_v(0, u, u, u)
            pool.wait_ge(ids_zero_out, 16)
            pool.wait_ge(place_step, PLACE_STEPS)
            for n in range(TILES):
                nc.gpsimd.indirect_dma_start(id_dram, bass.IndirectOffsetOnAxis(id_place[:, n:n + 1], 0), id_sb[:, n:n + 1],
                                             None).then_inc(ids_out, 16)
            pool.wait_ge(ids_in, 16)
            with pool.Fori(1, H // HEAD_BUFS) as j:
                take_body(0, j, j - 1)
            with pool.Fori(0, H // HEAD_BUFS - 1) as j:
                take_body(1, j, j + (H // HEAD_BUFS - 1))
            take_body(1, H // HEAD_BUFS - 1, BODIES - 2)
            for c in range(2):
                pool.wait_ge(y_stored[c], 16 * (1 + NT // 2))
            for n in range(TILES):
                nc.gpsimd.indirect_dma_start(ffn_sb[:, n, :], None, y_dram,
                                             bass.IndirectOffsetOnAxis(row_of[:, n:n + 1], 0)).then_inc(back_in, 16)
            pool.wait_ge(back_in, 16 * TILES)

        @block.scalar
        def _(act):
            def load_shift(slot, u):
                act.wait_ge(shift_read, slot + 1)
                for a in range(PARTS):
                    act.dma_start(q_st[u][RS + a:RS + a + 1, :].rearrange("a (t q) -> a t q", q=P),
                                  shift_rows[a * KT:(a + 1) * KT, :]).then_inc(shift_in, 16)

            def slot_work(slot, i, u):
                for kt in range(KT):
                    if kt >= P_BUFS:
                        act.wait_ge(pv_mm, slot * KT + kt - P_BUFS + 1)
                    for half in range(2):
                        act.wait_ge(st_mm, slot * 2 * KT + 2 * kt + half + 1)
                        nc.scalar.activation(probs[kt % P_BUFS][:, half * (L // 2):(half + 1) * (L // 2)], st_ps[half][:],
                                             ACT.Exp).then_inc(exp_done, 1)
                    if kt == TURN_AT + 1 and not known(slot, SLOTS - 1):
                        load_shift(slot + 1, (u + 1) % HEAD_BUFS)
                act.wait_ge(pv_mm, slot * KT + KT)
                nc.scalar.copy(o_acc[:], o_ps[:]).then_inc(o_read, 1)

            nc.scalar.activation(spare[:], ident_sb[:, 0:1], ACT.Exp)
            load_shift(0, 0)
            bodies(act, slot_work)

        @block.vector
        def _(dve):
            dve.sem_inc(ffn_done, BODY_TILES)

            def take_max(slot_base, k, maxima, qt, j):
                dve.wait_ge(wide_mm, slot_base + k + 1)
                nc.vector.tensor_reduce(maxima[:, qt, j:j + 1], wide_ps[k % WIDE][:], AX_X, ALU.max).then_inc(wide_read, 1)

            def shift_chain(step, slot, maxima, last_read):
                part = [shift[:, a * KT:(a + 1) * KT] for a in range(PARTS)]
                if step == 0:
                    dve.wait_ge(wide_read, last_read)
                    ins = nc.vector.tensor_reduce(neg_max[:], maxima[:], AX_X, ALU.max, negate=True)
                else:
                    dve.wait_ge(shift_step, slot * 6 + step)
                    if step == 1:
                        ins = nc.vector.tensor_copy(part[0], neg_max[:])
                    elif step == 2:
                        ins = nc.vector.tensor_tensor(shift_rest[:, 0, :], neg_max[:], part[0], ALU.subtract)
                    elif step == 3:
                        ins = nc.vector.tensor_copy(part[1], shift_rest[:, 0, :])
                    elif step == 4:
                        ins = nc.vector.tensor_tensor(shift_rest[:, 1, :], shift_rest[:, 0, :], part[1], ALU.subtract)
                    else:
                        ins = nc.vector.tensor_copy(part[2], shift_rest[:, 1, :])
                ins.then_inc(shift_step, 1)

            def take_shift(slot, use, k):
                if not known(slot, 0):
                    dve.wait_ge(shift_in, slot * 16 * PARTS)
                dve.wait_ge(wide_mm, use)
                nc.vector.tensor_copy(shift_rows[:], wide_ps[k % WIDE][:].bitcast(BF16)[0:SHIFT, 0:P]).then_inc(shift_read, 1)
                dve.wait_ge(shift_read, slot + 1)
                dve.sem_inc(wide_read, 1)

            def take_o(slot, use, k):
                turned = wide_ps[k % WIDE][:].rearrange("p (t d) -> p t d", d=VW)
                dve.wait_ge(wide_mm, use)
                nc.vector.reciprocal(rden[:], turned[:, :, DH]).then_inc(rden_done, 1)
                dve.wait_ge(rden_done, slot + 1)
                nc.vector.tensor_tensor(o_sb[:].rearrange("p (q c) n -> p c q n", c=KT // QC)[:, :, :, bass.ds(slot * DH, DH)],
                                        turned[:, :, 0:DH].rearrange("p (c q) d -> p c q d", q=QC),
                                        rden[:].rearrange("p (c q) -> p c q", q=QC).unsqueeze(3).broadcast_to([P, KT // QC, QC, DH]),
                                        ALU.mult).then_inc(wide_read, 1)

            def take_turned(use, k, c):
                dve.wait_ge(wide_mm, use)
                nc.vector.tensor_copy(xs_t[c % 2][:], wide_ps[k % WIDE][:, 0:D]).then_inc(wide_read, 1)

            def take_ffn(t, m, use, k, c):
                dve.wait_ge(wide_mm, use)
                dve.wait_ge(y_stored[c % 2], (m * (BODY_TILES // 2) + c // 2) * 16 + 16)
                nc.vector.tensor_tensor(y_tile[c % 2][:], wide_ps[k % WIDE][:, 0:D], b_tile[c][:], ALU.add).then_inc(ffn_done, 1)
                dve.wait_ge(ffn_done, t + 1 + BODY_TILES)
                dve.sem_inc(wide_read, 1)

            def dispatch_step(step):
                count = counts[:, TILES * T:COLS]
                upto = dispatch_sb[:, P:P + T * T].rearrange("p (e f) -> p e f", f=T)
                tile_row = dispatch_sb[:, P + T * T:P + T * T + NT]
                own_row = dispatch_sb[:, P + T * T + NT:P + T * T + NT + 1]
                if step:
                    dve.wait_ge(place_step, step)
                if step == 0:
                    dve.wait_ge(place_mm, 1)
                    ins = nc.vector.tensor_copy(counts[:], place_ps[:, 0:COLS])
                elif step == 1:
                    ins = nc.vector.tensor_scalar(over[:], count, float(P - 1), None, ALU.add)
                elif step == 2:
                    ins = nc.vector.tensor_scalar(tiles_of[:], over[:], LOG_P, None, ALU.arith_shift_right)
                elif step == 3:
                    ins = nc.vector.tensor_scalar(padded[:], tiles_of[:], float(P), None, ALU.mult)
                elif step == 4:
                    ins = nc.vector.tensor_tensor(upto_rows[:], padded[:].unsqueeze(1).broadcast_to([P, T, T]), upto, ALU.mult)
                elif step == 5:
                    ins = nc.vector.tensor_reduce(end_row[:], upto_rows[:], AX_X, ALU.add)
                elif step == 6:
                    ins = nc.vector.tensor_tensor(start_row[:], end_row[:], padded[:], ALU.subtract)
                elif step == 7:
                    ins = nc.vector.tensor_tensor(place[:], counts[:, 0:TILES * T].rearrange("p (n e) -> p n e", e=T),
                                                  start_row[:].unsqueeze(1).broadcast_to([P, TILES, T]), ALU.add)
                elif step == 8:
                    ins = nc.vector.tensor_tensor(place_own[:], place[:], onehot[:, 0:TILES, :], ALU.mult)
                elif step == 9:
                    ins = nc.vector.tensor_reduce(place_sum[:], place_own[:], AX_X, ALU.add)
                elif step == 10:
                    ins = nc.vector.tensor_copy(row_of[:], place_sum[:])
                elif step == 11:
                    ins = nc.vector.tensor_scalar(tile_of[:], row_of[:], LOG_P, None, ALU.arith_shift_right)
                elif step == 12:
                    ins = nc.vector.tensor_scalar(id_place_part[:], tile_of[:], float(1 - P * NT), None, ALU.mult)
                elif step == 13:
                    ins = nc.vector.scalar_tensor_tensor(id_place[:], place_sum[:], float(NT), id_place_part[:], ALU.mult, ALU.add)
                elif step == 14:
                    ins = nc.vector.tensor_tensor(past[:], end_row[:].unsqueeze(1).broadcast_to([P, NT, T]),
                                                  tile_row.unsqueeze(2).broadcast_to([P, NT, T]), ALU.is_le)
                elif step == 15:
                    ins = nc.vector.tensor_reduce(past_count[:], past[:], AX_X, ALU.add)
                elif step == 16:
                    ins = nc.vector.tensor_scalar(expert[:], past_count[:], float(T - 1), None, ALU.min)
                elif step == 17:
                    ins = nc.vector.tensor_scalar(tile_idx[:, :, 0:1].rearrange("p n a -> p (n a)"), expert[:], float(P), own_row, ALU.mult, ALU.add)
                else:
                    ins = nc.vector.tensor_copy(tile_idx[:, :, 1:2].rearrange("p n a -> p (n a)"), expert[:])
                ins.then_inc(place_step, 1)

            def slot_work(slot, i, u):
                first, k, maxima = base(slot, i, u), 0, chunk_max[(u + 1) % 2]
                ffn = ffn_tiles(slot, i, u)
                last_read = None
                for kt in range(KT):
                    ahead, qt = target(kt)
                    for j in range(QC):
                        if searched(slot, kt):
                            take_max(first, k, chunk_max[(u + ahead) % 2], qt, j)
                            k += 1
                        if known(slot, 0) and kt * QC + j + 1 < PLACE_STEPS:
                            dispatch_step(kt * QC + j + 1)
                        step = (kt - (KT - LEAD)) * QC + j
                        if 0 <= step < 6 and not known(slot, SLOTS - 1):
                            shift_chain(step, slot + 1, maxima, last_read)
                    if kt == KT - LEAD - 1:
                        last_read = first + k
                    if kt == O_AT and not known(slot, 0):
                        take_o(slot - 1, first + k + 1, k)
                        k += 1
                    for n, c in enumerate(ffn):
                        if kt == FFN_TURN_AT[n]:
                            take_turned(first + k + 1, k, c)
                            k += 1
                        if kt == FFN_AT[n]:
                            take_ffn((i - 1) * BODY_TILES + c, i - 1, first + k + 1, k, c)
                            k += 1
                    if kt == TURN_AT and not known(slot, SLOTS - 1):
                        take_shift(slot + 1, first + k + 1, k)
                        k += 1

            k = 0
            for qt in range(EARLY, KT + LEAD):
                for j in range(QC):
                    take_max(0, k, chunk_max[qt // KT], qt % KT, j)
                    k += 1
                if qt == EARLY + TILES // QC:
                    dispatch_step(0)
                if qt == KT - 1:
                    for step in range(6):
                        shift_chain(step, 0, chunk_max[0], k)
                if qt == KT:
                    take_shift(0, k + 1, k)
                    k += 1
            bodies(dve, slot_work)
            take_o(SLOTS - 1, base(SLOTS, BODIES, 0) + 1, 0)

        @block.tensor
        def _(pe):
            def search(k, n, qt, j):
                nc.tensor.matmul(wide_ps[k % WIDE][:], q_st[n][0:RS, qt * P:(qt + 1) * P], k_st[n][0:RS, j * 512:(j + 1) * 512],
                                 start=True, stop=True).then_inc(wide_mm, 1)

            def scores(slot, u, kt, half):
                if known(slot, 0) and kt == half == 0:
                    pe.wait_ge(place_step, 1)
                if not (known(slot, 0) and kt == 0):
                    pe.wait_ge(exp_done, slot * 2 * KT + 2 * kt + half - 1)
                for c in range(2):
                    q0 = half * (L // 2) + c * 512
                    last = nc.tensor.matmul(st_ps[half][:, c * 512:(c + 1) * 512], k_st[u][0:RA, kt * P:(kt + 1) * P],
                                            q_st[u][0:RA, q0:q0 + 512], start=True, stop=True)
                last.then_inc(st_mm, 1)

            def values(slot, u, kt):
                if kt == 0:
                    if not known(slot, 0):
                        pe.wait_ge(o_read, slot)
                    pe.wait_ge(vh_done, slot + 1)
                pe.wait_ge(exp_done, slot * 2 * KT + 2 * kt + 2)
                for c in range(QC):
                    last = nc.tensor.matmul(o_ps[VW * c:VW * (c + 1), :], vh[u][:, kt, :], probs[kt % P_BUFS][:, c * 512:(c + 1) * 512],
                                            start=(kt == 0), stop=(kt == KT - 1), tile_position=(0, VW * c))
                last.then_inc(pv_mm, 1)

            def turn_shift(slot, k):
                pe.wait_ge(shift_step, slot * 6 + 6)
                nc.tensor.transpose(wide_ps[k % WIDE][:].bitcast(BF16)[:, 0:P], shift[:], ident_bf[:]).then_inc(wide_mm, 1)

            def turn_o(slot, k):
                pe.wait_ge(o_read, slot + 1)
                for c in range(KT // QC):
                    mm = nc.tensor.transpose(wide_ps[k % WIDE][:, c * P:(c + 1) * P], o_acc[:, c * P:(c + 1) * P], ident_sb[:])
                mm.then_inc(wide_mm, 1)

            def turn_tokens(m, k, c):
                pe.wait_ge(fetch_in[c], (m + 1) * 16 * FETCHES)
                for a in range(KD):
                    mm = nc.tensor.transpose(wide_ps[k % WIDE][:, a * P:(a + 1) * P],
                                             xs[c][:].rearrange("p (q k) -> p k q", k=KD)[:, a, :], ident_sb[:])
                mm.then_inc(wide_mm, 1)

            def feed_forward(k, c, turned):
                pe.wait_ge(wide_read, turned)
                for a in range(KD):
                    mm = nc.tensor.matmul(wide_ps[k % WIDE][:, 0:D], xs_t[c % 2][:, a * P:(a + 1) * P], w_tile[c][:, a * D:(a + 1) * D],
                                          start=(a == 0), stop=(a == KD - 1))
                mm.then_inc(wide_mm, 1)

            def slot_work(slot, i, u):
                k = 0
                ffn = ffn_tiles(slot, i, u)
                turned = None
                pe.wait_ge(shift_in, (slot + 1) * 16 * PARTS)
                for kt in range(KT):
                    ahead, qt = target(kt)
                    n = (u + ahead) % HEAD_BUFS
                    if qt == 0 and searched(slot, kt):
                        pe.wait_ge(stack_in[n], (i + (u + ahead) // HEAD_BUFS + 1) * 16 * LOADS)
                    for j in range(QC):
                        if searched(slot, kt):
                            pe.wait_ge(wide_read, free_at(slot, i, u, k))
                            search(k, n, qt, j)
                            k += 1
                        if j < 2:
                            scores(slot, u, kt, j)
                        if j == 2 and kt:
                            values(slot, u, kt - 1)
                    if kt == O_AT and not known(slot, 0):
                        pe.wait_ge(wide_read, free_at(slot, i, u, k))
                        turn_o(slot - 1, k)
                        k += 1
                    for n, c in enumerate(ffn):
                        if kt == FFN_TURN_AT[n]:
                            pe.wait_ge(wide_read, free_at(slot, i, u, k))
                            turn_tokens(i - 1, k, c)
                            k += 1
                            turned = base(slot, i, u) + k
                        if kt == FFN_AT[n]:
                            pe.wait_ge(wide_read, free_at(slot, i, u, k))
                            feed_forward(k, c, turned)
                            k += 1
                    if kt == TURN_AT and not known(slot, SLOTS - 1):
                        pe.wait_ge(wide_read, free_at(slot, i, u, k))
                        turn_shift(slot + 1, k)
                        k += 1
                values(slot, u, KT - 1)

            nc.tensor.matmul(place_ps[:, 0:COLS], before[:], onehot[:], start=True, stop=False)

            def count_tile(n):
                mm = nc.tensor.matmul(place_ps[:, (n + 1) * T:COLS], ones[:], onehot[:, n:n + 1, :].broadcast_to([P, TILES - n, T]),
                                      start=False, stop=(n == TILES - 1))
                if n == TILES - 1:
                    mm.then_inc(place_mm, 1)

            k = 0
            for qt in range(EARLY, KT + LEAD):
                if qt in (EARLY, KT):
                    pe.wait_ge(stack_in[qt // KT], 16 * LOADS)
                for j in range(QC):
                    if k >= WIDE:
                        pe.wait_ge(wide_read, k - WIDE + 1)
                    search(k, qt // KT, qt % KT, j)
                    if (qt - EARLY) * QC + j < TILES:
                        count_tile((qt - EARLY) * QC + j)
                    k += 1
                if qt == KT:
                    pe.wait_ge(wide_read, k - WIDE + 1)
                    turn_shift(0, k)
                    k += 1
            bodies(pe, slot_work)
            pe.wait_ge(wide_read, base(SLOTS, BODIES, 0))
            turn_o(SLOTS - 1, 0)


def stage_c(nc, x, out, o_sb, ffn_sb, ident_sb, wout_sb, bout_row):
    BUFS = 4
    AHEAD = 2
    with ExitStack() as ctx:
        def sb(name, shape, dt=F32):
            return ctx.enter_context(nc.sbuf_tensor(name, shape, dt))

        def sem(name):
            return ctx.enter_context(nc.semaphore(name))

        x_sb = [sb(f"xc_sb{i}", [P, D]) for i in range(2 * BUFS)]
        o_tile = [sb(f"o_tile{i}", [P, D]) for i in range(BUFS)]
        ot_sb = [sb(f"ot_sb{i}", [P, D]) for i in range(BUFS)]
        part_sum = [sb(f"part_sum{i}", [P, D]) for i in range(BUFS)]
        y_sb = [sb(f"y_sb{i}", [P, D]) for i in range(2 * BUFS)]
        ot_ps = [ctx.enter_context(nc.psum_tensor(f"ot_ps{i}", [P, 512], F32)) for i in range(BUFS)]
        y_ps = [ctx.enter_context(nc.psum_tensor(f"y_ps{i}", [P, 512], F32)) for i in range(BUFS)]
        x_in = [sem(f"xc_in{i}") for i in range(2 * BUFS)]
        y_out = [sem(f"y_out{i}") for i in range(2 * BUFS)]
        tile_done = sem("tile_done")
        ot_mm = sem("ot_mm")
        ot_done = sem("ot_done")
        y_mm = sem("y_mm")
        sum_done = sem("sum_done")
        xb_done = sem("xb_done")
        y_done = sem("y_done")
        x_rows = x.rearrange("b (t p) d -> (b t) p d", p=P)
        out_rows = out.rearrange("b (t p) d -> (b t) p d", p=P)
        TURN = 2 * BUFS
        block = ctx.enter_context(nc.Block())

        @block.sync
        def _(sp):
            for c in range(TURN):
                sp.sem_inc(y_out[c], 16)

            def load(n, c):
                sp.dma_start(x_sb[c][:], x_rows[bass.ds(n, 1)].rearrange("a p d -> (a p) d")).then_inc(x_in[c], 16)

            def store(n, c):
                sp.wait_ge(y_done, n + BUFS + 1)
                sp.dma_start(out_rows[bass.ds(n, 1)].rearrange("a p d -> (a p) d"), y_sb[c][:]).then_inc(y_out[c], 16)

            for c in range(TURN):
                load(c, c)
            with sp.Fori(0, TILES // TURN - 1) as i:
                for c in range(TURN):
                    store(i * TURN + c, c)
                    load(i * TURN + TURN + c, c)
            for c in range(TURN):
                store(TILES - TURN + c, c)
            for c in range(TURN):
                sp.wait_ge(y_out[c], 16 * (1 + TILES // TURN))

        @block.scalar
        def _(act):
            act.sem_inc(ot_done, BUFS)

            def gather_tile(n, c, b, t):
                act.wait_ge(ot_mm, n + 1)
                nc.scalar.copy(o_tile[c % BUFS][:],
                               o_sb[:, bass.ds(t, 1), b * D:(b + 1) * D].rearrange("p a d -> p (a d)")).then_inc(tile_done, 1)

            def copy_turned(n, c):
                act.wait_ge(ot_mm, n + BUFS + 1)
                act.wait_ge(y_mm, n + 1)
                nc.scalar.copy(ot_sb[c % BUFS][:], ot_ps[c % BUFS][:, 0:D]).then_inc(ot_done, 1)

            for b in range(B):
                with act.Fori(0, KT // TURN) as r:
                    for c in range(TURN):
                        n = r * TURN + (b * KT + c)
                        gather_tile(n, c, b, r * TURN + c)
                        if c:
                            copy_turned(n - 1, c - 1)
                    copy_turned(n, c)

        @block.gpsimd
        def _(pool):
            pool.sem_inc(xb_done, BUFS)

            with pool.Fori(0, TILES // TURN) as r:
                for c in range(TURN):
                    pool.wait_ge(x_in[c], r * 16 + 16)
                    nc.gpsimd.tensor_tensor(x_sb[c][:], x_sb[c][:], bout_row[:], ALU.add).then_inc(xb_done, 1)

        @block.tensor
        def _(pe):
            pe.sem_inc(ot_mm, BUFS)
            pe.sem_inc(y_mm, BUFS)

            def turn(n, c):
                pe.wait_ge(tile_done, n + 1)
                pe.wait_ge(ot_done, n + 1)
                for k in range(KD):
                    last = nc.tensor.transpose(ot_ps[c % BUFS][:, k * P:(k + 1) * P], o_tile[c % BUFS][:, k * P:(k + 1) * P],
                                               ident_sb[:])
                last.then_inc(ot_mm, 1)

            def project(n, c):
                pe.wait_ge(ot_done, n + BUFS + 1)
                pe.wait_ge(sum_done, n + 1)
                for k in range(KD):
                    last = nc.tensor.matmul(y_ps[c % BUFS][:, 0:D], ot_sb[c % BUFS][:, k * P:(k + 1) * P], wout_sb[:, k, :],
                                            start=(k == 0), stop=(k == KD - 1))
                last.then_inc(y_mm, 1)

            for c in range(AHEAD):
                turn(c, c)
            with pe.Fori(0, TILES // BUFS - 1) as i:
                for c in range(BUFS):
                    turn(i * BUFS + c + AHEAD, c + AHEAD)
                    project(i * BUFS + c, c)
            for c in range(BUFS):
                if c + AHEAD < BUFS:
                    turn(TILES - BUFS + c + AHEAD, c + AHEAD)
                project(TILES - BUFS + c, c)

        @block.vector
        def _(dve):
            dve.sem_inc(sum_done, BUFS)
            dve.sem_inc(y_done, BUFS)

            def add_ffn(n, c):
                dve.wait_ge(y_mm, n + BUFS + 1)
                dve.wait_ge(y_done, n + 1)
                nc.vector.tensor_tensor(part_sum[c % BUFS][:], y_ps[c % BUFS][:, 0:D],
                                        ffn_sb[:, bass.ds(n, 1), :].rearrange("p a d -> p (a d)"), ALU.add).then_inc(sum_done, 1)

            def add_x(n, turn, c):
                dve.wait_ge(sum_done, n + BUFS + 1)
                dve.wait_ge(xb_done, n + BUFS + 1)
                dve.wait_ge(y_out[c], turn * 16 + 16)
                nc.vector.tensor_tensor(y_sb[c][:], part_sum[c % BUFS][:], x_sb[c][:], ALU.add).then_inc(y_done, 1)

            with dve.Fori(0, TILES // TURN) as r:
                for c in range(TURN + 1):
                    if c < TURN:
                        add_ffn(r * TURN + c, c)
                    if c:
                        add_x(r * TURN + c - 1, r, c - 1)


_INS = ["L0_attn_x", "L0_attn_w_qkv", "L0_attn_b_qkv", "L0_attn_w_out", "L0_attn_b_out", "L0_ffn_tile_sigs", "L0_ffn_W",
        "L0_ffn_b"]


def kernel(**inputs):
    import numpy as _np
    import concourse.bacc as _bacc
    from concourse import mybir as _mybir
    from concourse.bass_utils import run_bass_kernel_spmd as _run

    nc = _bacc.Bacc("TRN2", target_bir_lowering=False, num_devices=1)
    arrays, args = {}, []

    def give(name, a):
        a = _np.ascontiguousarray(a)
        arrays[name] = a
        args.append(nc.dram_tensor(name, a.shape, _mybir.dt.from_np(a.dtype), kind="ExternalInput").ap())

    for name in _INS:
        give(f"in_{name}_dram", inputs[name].T if name == "L0_ffn_tile_sigs" else inputs[name])
    give("in_bqk_cols_dram", _np.asarray(inputs["L0_attn_b_qkv"])[0:2 * D].reshape(MB, P).T)
    for name, a in zip(("rope", "ident", "swap", "rank", "dispatch", "token_id"), build_tables()):
        give(f"table_{name}_dram", a)
    out = nc.dram_tensor("out_dram", (B, L, D), _mybir.dt.float32, kind="ExternalOutput").ap()
    routed_attention_kernel(nc, *args, out)
    r = _run(nc, [arrays], core_ids=[0])
    return r.results[0]["out_dram"]
```
